# Optimizing a Trainium2 kernel written in Bass

```python
import numpy as np
import jax
import jax.numpy as jnp

def _softmax(x, axis=-1):
    return jax.nn.softmax(x, axis=axis)

def _gelu(x):
    return jax.nn.gelu(x, approximate=True)

def _silu(x):
    return jax.nn.silu(x)

def _sigmoid(x):
    return jax.nn.sigmoid(x)

def _layernorm(x, axis=-1, eps=1e-05):
    m = jnp.mean(x, axis=axis, keepdims=True)
    v = jnp.var(x, axis=axis, keepdims=True)
    return (x - m) / jnp.sqrt(v + eps)

def _scatter_add(tgt, idx, src, axis=0):
    return tgt.at[idx].add(src)

def _segment_sum(src, seg, n):
    return jax.ops.segment_sum(src, seg, n)
kernel_name = 'mk_flamingo_gated_d1_seqx_r4_e49694'

def setup_inputs(seed: int=0):
    np.random.seed(seed)
    _w = jnp.asarray

    def _rec_inputs():
        import jax
        import jax.numpy as jnp
        _rk = jax.random.key(seed)
        x = -0.0002928 + 1 * jax.random.normal(jax.random.fold_in(_rk, 1), (16, 128, 256), jnp.float32)
        _lenS = 128 - jax.random.randint(jax.random.fold_in(_rk, 7), (16,), 0, max(1, 128 // 4) + 1, jnp.int32)
        _lenS2 = 128 - jax.random.randint(jax.random.fold_in(_rk, 8), (16,), 0, max(1, 128 // 4) + 1, jnp.int32)
        _ctx_1024P = jax.random.normal(jax.random.fold_in(_rk, 11), (16, 16, 256), jnp.float32)
        _ctx_1024c = jax.random.dirichlet(jax.random.fold_in(_rk, 511), 0.3 * jnp.ones((16,), jnp.float32), (16, 128))
        _ctx_1024t = jnp.einsum('bsk,bkd->bsd', _ctx_1024c, _ctx_1024P)
        _ctx_1024t = _ctx_1024t * jax.lax.rsqrt(jnp.mean(jnp.square(_ctx_1024t)) + 1e-12) * 0.953939
        ctx_1024 = -1.39393e-06 + 0.999914 * (_ctx_1024t + 0.3 * jax.random.normal(jax.random.fold_in(_rk, 611), (16, 128, 256), jnp.float32))
        fside_BxS2_0 = jax.random.uniform(jax.random.fold_in(_rk, 12), (16, 128), jnp.float32, 0.0, 0.999833)
        _g = jax.random.normal(jax.random.fold_in(_rk, 9001), (2, 1), jnp.float32)
        _g = jnp.sign(_g) * jnp.maximum(jnp.abs(_g), 1.0) + (_g == 0) * 1.0
        g_xattn = _g[0]
        g_ffn = _g[1]
        return (x, ctx_1024, fside_BxS2_0, g_xattn, g_ffn)
    x, ctx_1024, fside_BxS2_0, g_xattn, g_ffn = _rec_inputs()

    def _L0_xattn_setup():
        import jax, jax.numpy as jnp
        import numpy as np
        D_MODEL = 256
        NHEAD = 16
        HEAD_DIM = D_MODEL // NHEAD
        CLAMP_MIN = -0.2
        CLAMP_MAX = 0.2
        key = jax.random.key(seed)
        ks = jax.random.split(key, 16)
        B, T = (2, 512)
        s = 1.0 / np.sqrt(D_MODEL)
        inp = {'query': jax.random.normal(ks[0], (B, T, D_MODEL), jnp.float32), 'key': jax.random.normal(ks[1], (B, T, D_MODEL), jnp.float32), 'value': jax.random.normal(ks[2], (B, T, D_MODEL), jnp.float32), 'frac': jax.random.uniform(ks[3], (B, T), jnp.float32), 'Wq': jax.random.normal(ks[4], (D_MODEL, D_MODEL), jnp.float32) * s, 'bq': jnp.zeros((D_MODEL,), jnp.float32), 'Wk': jax.random.normal(ks[5], (D_MODEL, D_MODEL), jnp.float32) * s, 'bk': jnp.zeros((D_MODEL,), jnp.float32), 'Wv': jax.random.normal(ks[6], (D_MODEL, D_MODEL), jnp.float32) * s, 'bv': jnp.zeros((D_MODEL,), jnp.float32), 'Wo': jax.random.normal(ks[7], (D_MODEL, D_MODEL), jnp.float32) * s, 'bo': jnp.zeros((D_MODEL,), jnp.float32), 'alpha_pos': jax.random.normal(ks[8], (NHEAD,), jnp.float32) * 0.1, 'alpha_neg': jax.random.normal(ks[9], (NHEAD,), jnp.float32) * 0.1, 'gamma': jnp.float32(1.0), 'delta': jnp.float32(1.0)}
        return inp
    _L0_xattn_all = _L0_xattn_setup()
    _L0_xattn_in = {k: v for k, v in _L0_xattn_all.items() if k in ('Wq', 'bq', 'Wk', 'bk', 'Wv', 'bv', 'Wo', 'bo', 'alpha_pos', 'alpha_neg', 'gamma', 'delta')}
    del _L0_xattn_all

    def _L0_ffn_setup():
        import jax, jax.numpy as jnp
        import numpy as np
        B, S, DIM = (4, 512, 256)
        E, K, HID = (8, 2, 1024)
        key = jax.random.key(seed)
        ks = jax.random.split(key, 8)
        init = lambda k, sh: jax.random.normal(k, sh, jnp.float32) * 0.02
        return {'x': jax.random.normal(ks[0], (B, S, DIM), jnp.float32), 'gate_w': init(ks[1], (DIM, E)), 'gate_b': jnp.zeros((E,), jnp.float32), 'w1': init(ks[2], (E, DIM, HID)), 'b1': jnp.zeros((E, HID), jnp.float32), 'w2': init(ks[3], (E, HID, DIM)), 'b2': jnp.zeros((E, DIM), jnp.float32), 'ws1': init(ks[4], (DIM, HID)), 'bs1': jnp.zeros((HID,), jnp.float32), 'ws2': init(ks[5], (HID, DIM)), 'bs2': jnp.zeros((DIM,), jnp.float32)}
    _L0_ffn_all = _L0_ffn_setup()
    _L0_ffn_in = {k: v for k, v in _L0_ffn_all.items() if k in ('gate_w', 'gate_b', 'w1', 'b1', 'w2', 'b2', 'ws1', 'bs1', 'ws2', 'bs2')}
    del _L0_ffn_all
    return {'x': x, 'ctx_1024': ctx_1024, 'fside_BxS2_0': fside_BxS2_0, 'g_xattn': g_xattn, 'g_ffn': g_ffn, 'L0_xattn_Wq': _L0_xattn_in['Wq'], 'L0_xattn_bq': _L0_xattn_in['bq'], 'L0_xattn_Wk': _L0_xattn_in['Wk'], 'L0_xattn_bk': _L0_xattn_in['bk'], 'L0_xattn_Wv': _L0_xattn_in['Wv'], 'L0_xattn_bv': _L0_xattn_in['bv'], 'L0_xattn_Wo': _L0_xattn_in['Wo'], 'L0_xattn_bo': _L0_xattn_in['bo'], 'L0_xattn_alpha_pos': _L0_xattn_in['alpha_pos'], 'L0_xattn_alpha_neg': _L0_xattn_in['alpha_neg'], 'L0_xattn_gamma': _L0_xattn_in['gamma'], 'L0_xattn_delta': _L0_xattn_in['delta'], 'L0_ffn_gate_w': _L0_ffn_in['gate_w'], 'L0_ffn_gate_b': _L0_ffn_in['gate_b'], 'L0_ffn_w1': _L0_ffn_in['w1'], 'L0_ffn_b1': _L0_ffn_in['b1'], 'L0_ffn_w2': _L0_ffn_in['w2'], 'L0_ffn_b2': _L0_ffn_in['b2'], 'L0_ffn_ws1': _L0_ffn_in['ws1'], 'L0_ffn_bs1': _L0_ffn_in['bs1'], 'L0_ffn_ws2': _L0_ffn_in['ws2'], 'L0_ffn_bs2': _L0_ffn_in['bs2']}

def reference(x, ctx_1024, fside_BxS2_0, g_xattn, g_ffn, L0_xattn_Wq, L0_xattn_bq, L0_xattn_Wk, L0_xattn_bk, L0_xattn_Wv, L0_xattn_bv, L0_xattn_Wo, L0_xattn_bo, L0_xattn_alpha_pos, L0_xattn_alpha_neg, L0_xattn_gamma, L0_xattn_delta, L0_ffn_gate_w, L0_ffn_gate_b, L0_ffn_w1, L0_ffn_b1, L0_ffn_w2, L0_ffn_b2, L0_ffn_ws1, L0_ffn_bs1, L0_ffn_ws2, L0_ffn_bs2):
    import jax
    import jax.numpy as jnp

    def _L0_xattn_ref(query, key, value, frac, Wq, bq, Wk, bk, Wv, bv, Wo, bo, alpha_pos, alpha_neg, gamma, delta):
        import jax, jax.numpy as jnp
        import numpy as np
        D_MODEL = 256
        NHEAD = 16
        HEAD_DIM = D_MODEL // NHEAD
        CLAMP_MIN = -0.2
        CLAMP_MAX = 0.2
        B, T, _ = query.shape
        scale = HEAD_DIM ** (-0.5)

        def proj(x, W, b):
            y = x @ W.T + b
            return y.reshape(B, T, NHEAD, HEAD_DIM).transpose(0, 2, 1, 3)
        Q = proj(query, Wq, bq)
        K = proj(key, Wk, bk)
        V = proj(value, Wv, bv)
        logits = jnp.einsum('bhqd,bhkd->bhqk', Q, K) * scale
        D = jnp.clip(frac[:, None, :] - frac[:, :, None], CLAMP_MIN, CLAMP_MAX)
        D_pos = jnp.maximum(D, 0.0)
        D_neg = jnp.minimum(D, 0.0)
        ap = alpha_pos[None, :, None, None]
        an = alpha_neg[None, :, None, None]
        stoich_bias = ap * D_pos[:, None] + an * D_neg[:, None]
        attn = gamma * logits + delta * stoich_bias
        probs = jax.nn.softmax(attn, axis=-1)
        out = jnp.einsum('bhqk,bhkd->bhqd', probs, V)
        out = out.transpose(0, 2, 1, 3).reshape(B, T, D_MODEL)
        return out @ Wo.T + bo

    def _L0_ffn_ref(x, gate_w, gate_b, w1, b1, w2, b2, ws1, bs1, ws2, bs2):
        import jax, jax.numpy as jnp
        import numpy as np
        B, S, DIM = (4, 512, 256)
        E, K, HID = (8, 2, 1024)
        orig_shape = x.shape
        xf = x.reshape(-1, DIM)
        logits = xf @ gate_w + gate_b
        top_w, top_i = jax.lax.top_k(logits, K)
        gw = jax.nn.softmax(top_w, axis=-1).astype(xf.dtype)
        combine = (gw[:, :, None] * jax.nn.one_hot(top_i, E, dtype=xf.dtype)).sum(axis=1)
        out = jnp.zeros_like(xf)
        for e in range(E):
            h = jax.nn.gelu(xf @ w1[e] + b1[e], approximate=False)
            out = out + combine[:, e:e + 1] * (h @ w2[e] + b2[e])
        shared = jax.nn.gelu(xf @ ws1 + bs1, approximate=False) @ ws2 + bs2
        return (out + shared).reshape(orig_shape)
    x = x + jnp.tanh(g_xattn[0]) * _L0_xattn_ref(_layernorm(x, axis=-1), ctx_1024, ctx_1024, fside_BxS2_0, L0_xattn_Wq, L0_xattn_bq, L0_xattn_Wk, L0_xattn_bk, L0_xattn_Wv, L0_xattn_bv, L0_xattn_Wo, L0_xattn_bo, L0_xattn_alpha_pos, L0_xattn_alpha_neg, L0_xattn_gamma, L0_xattn_delta)
    x = x + jnp.tanh(g_ffn[0]) * _L0_ffn_ref(_layernorm(x, axis=-1), L0_ffn_gate_w, L0_ffn_gate_b, L0_ffn_w1, L0_ffn_b1, L0_ffn_w2, L0_ffn_b2, L0_ffn_ws1, L0_ffn_bs1, L0_ffn_ws2, L0_ffn_bs2)
    return x

_drawn_inputs = setup_inputs


def setup_inputs(seed=0):
    import zlib

    import numpy as np

    out = dict(_drawn_inputs(seed))
    spreads = {'L0_xattn_bq': (0.0, 0.373),
     'L0_xattn_bk': (0.0, 2.0),
     'L0_xattn_bv': (0.0, 0.1),
     'L0_xattn_bo': (0.0, 0.1),
     'L0_ffn_gate_b': (0.0, 0.1),
     'L0_ffn_b1': (0.0, 0.357),
     'L0_ffn_b2': (0.0, 0.1),
     'L0_ffn_bs1': (0.0, 0.281),
     'L0_ffn_bs2': (0.0, 0.1)}
    factors = {'fside_BxS2_0': 36.744, 'L0_xattn_alpha_pos': 45.449, 'L0_xattn_alpha_neg': 42.115}
    for name, (base, spread) in spreads.items():
        noise = np.random.default_rng([zlib.crc32(name.encode()), seed]).standard_normal(out[name].shape)
        drawn = base * np.exp(spread * noise) if base else spread * noise
        out[name] = jnp.asarray(drawn.astype(out[name].dtype))
    for name, factor in factors.items():
        out[name] = (out[name] * factor).astype(out[name].dtype)
    return out
```

```python
import concourse.bass as bass
from concourse import mybir
from contextlib import ExitStack

P = 128
B, T, D = 16, 128, 256
H, HD = 16, 16
E, HID = 8, 1024
N = B * T
DC = D // P
HC = HID // P
R = 4
HR = H // R
STEPS = B * R
PAIRS = B // 2
TOPK = 2
SLOTS = N * TOPK // P + E - 1
GROUPS = N // 512
CLAMP = 0.2
EPS = 1e-5
ROW = D + 2

WS = 2 * 2 * DC * HID
W1H, W1L, W2H, W2L = (k * DC * HID for k in range(4))
EARLY = 6

C_ID, C_UP = 0, P
C_EVEN, C_ODD, C_R0, C_R1, C_R01 = (2 * P + k for k in range(5))
C_IOTA = 2 * P + 5
C_TOK = C_IOTA + E
C_PAD = C_TOK + B
C_TILE = C_PAD + 1
C_N = C_TILE + SLOTS
K_BQ, K_BK, K_BV, K_FR = 0, DC, 2 * DC, 3 * DC
K_BS1 = K_FR + B
K_B1 = K_BS1 + HC
K_GW = K_B1 + E * HC
K_N = K_GW + DC * E
V_AP, V_AN, V_GAMMA, V_DELTA, V_GX, V_GF = 0, H, 2 * H, 2 * H + 1, 2 * H + 2, 2 * H + 3
V_GB = 2 * H + 4
V_BO = V_GB + E
V_BS2 = V_BO + D
V_N = V_BS2 + D


def head(r, j):
    return 8 * (j // 2) + 2 * r + j % 2


def build(nc, x, ctxT, frac, wproj, consts, cols, rows, b2, w1, w2, xs_dram, out):
    fp32, bf16 = mybir.dt.float32, mybir.dt.bfloat16
    i32, u32 = mybir.dt.int32, mybir.dt.uint32
    ALU, ACT, AX = mybir.AluOpType, mybir.ActivationFunctionType, mybir.AxisListType

    with ExitStack() as ctx:
        def sb(name, shape, dt=fp32):
            return ctx.enter_context(nc.sbuf_tensor(name, shape, dt))

        def sem(name):
            return ctx.enter_context(nc.semaphore(name))

        W = sb("W", [P, (1 + E) * WS], bf16)
        xres = sb("xres", [P, B * D])
        xT2 = sb("xT2", [P, 2 * DC * N], bf16)
        stage = sb("stage", [P, 2 * HID])
        hbuf = sb("hbuf", [P, 2, 512])
        hsplit = sb("hsplit", [P, 2, 2, 512], bf16)
        pay = sb("pay", [P, 2, TOPK, ROW])
        b2hl = sb("b2hl", [P, E * D], bf16)
        cst = sb("cst", [P, C_N])
        col = sb("col", [P, K_N])
        row = sb("row", [P, V_N])
        upb = sb("upb", [P, P], bf16)
        oneb = sb("oneb", [P, P], bf16)
        selb = sb("selb", [P, P], bf16)
        gwhl = sb("gwhl", [P, 2, DC, E], bf16)
        ident = cst[:, C_ID:C_ID + P]

        top = [EARLY * WS]

        def under(n, dt=fp32):
            size = n * (2 if dt == fp32 else 1)
            at = top[0]
            top[0] += size
            assert top[0] <= (1 + E) * WS
            v = W[:, at:at + size]
            return v.bitcast(fp32) if dt == fp32 else v

        sc = [under(HR * T) for _ in range(R)]
        pb = [under(HR * T) for _ in range(R)]
        pth = [under(HR * T, bf16) for _ in range(2)]
        ptl = [under(HR * T, bf16) for _ in range(2)]
        qT = [under(DC * T) for _ in range(2)]
        kz = [under(2 * DC * T) for _ in range(2)]
        vh = [under(D, bf16) for _ in range(2)]
        vl = [under(D, bf16) for _ in range(2)]
        cT = [under(DC * T) for _ in range(2)]
        xh = under(D)
        xhT = under(DC * T)
        on = under(D)
        oT = under(DC * T)
        fr = [under(T) for _ in range(2)]
        dneg = [under(T) for _ in range(2)]
        dd = under(T)
        dpos = under(T)
        wp = under(4 * DC * D)
        bo_t = under(D)

        def wproj_at(k, c):
            return wp[:, (k * DC + c) * D:(k * DC + c + 1) * D]

        xs = [stage[:, k * ROW:(k + 1) * ROW] for k in range(2)]
        hs = [xT2[:, k * 2048:(k + 1) * 2048] for k in range(2)]
        xsT = [xT2[:, 4096 + k * 512:4096 + (k + 1) * 512] for k in range(2)]
        ysb = [xT2[:, 5120 + k * 512:5120 + (k + 1) * 512].bitcast(fp32) for k in range(2)]

        def pt(name, shape, dt=fp32):
            return sb(name, shape, dt)
        st6 = pt("st6", [P, B, 6])
        mv1 = pt("mv1", [P, B, 2])
        mv2 = pt("mv2", [P, B, 2])
        rstd1 = pt("rstd1", [P, B])
        rstd2 = pt("rstd2", [P, B])
        mhalf = pt("mhalf", [P, B])
        mn = pt("mn", [P, 2, H])
        sm = pt("sm", [P, 2, H])
        rs = pt("rs", [P, H])
        tgx = pt("tgx", [P, 1])
        tgf = pt("tgf", [P, 1])
        gs = pt("gs", [P, 1])
        bqs = pt("bqs", [P, DC])
        bkm = pt("bkm", [P, 2, DC])
        apd = pt("apd", [P, H])
        and_ = pt("and_", [P, H])
        bs2t = row[:, V_BS2:V_BS2 + D]
        parts = hsplit[:].rearrange("p a b n -> p (a b n)")
        lg, mx8, ix8f, oh0, oh1, ca0, ca1, offs = (
            parts[:, k * 256:(k + 1) * 256].bitcast(fp32).rearrange("p (b e) -> p b e", e=E) for k in range(8))
        ix8 = parts[:, 512:768].bitcast(u32).rearrange("p (b e) -> p b e", e=E)
        oh, ca = [oh0, oh1], [ca0, ca1]
        tcmp = hbuf[:].rearrange("p a n -> p (a n)")[:, 0:SLOTS * E].rearrange("p (j e) -> p j e", e=E)
        ixf = pt("ixf", [P, B, TOPK])
        wt = pt("wt", [P, B, TOPK])
        wid = pt("wid", [P, B, TOPK, 2])
        ed = pt("ed", [P, B])
        wx = pt("wx", [P, 2, 1])
        posf = pt("posf", [P, TOPK, B])
        posu = pt("posu", [P, TOPK, B], u32)
        place = pt("place", [P, 2, TOPK], u32)
        selm = (hbuf[:].rearrange("p a n -> p (a n)")[:, 512:512 + B * E // 2].bitcast(bf16)
                .rearrange("p (b e) -> p b e", e=E))
        te_i = pt("te_i", [P, E], i32)
        te = [pt(f"te{k}", [P, E]) for k in range(3)]
        tef = pt("tef", [P, SLOTS])
        tei = pt("tei", [P, SLOTS], i32)
        b1t = pt("b1t", [P, 2, HC])
        idu = pt("idu", [P, 2, 1], u32)
        padt = pay[:, 0, 0, :]

        bank = [ctx.enter_context(nc.psum_tensor(f"bank{k}", [P, 512], fp32)) for k in range(8)]
        psS, psT, psQK, psO, psM, psVY = bank[0:2], bank[2:4], bank[4], bank[5], bank[6], bank[7]

        ld_par, ld_wp, ld_b2 = sem("ld_par"), sem("ld_wp"), sem("ld_b2")
        ld_x = [sem(f"ld_x{k}") for k in range(4)]
        ld_ctx = [sem(f"ld_ctx{k}") for k in range(2)]
        ld_st = [sem(f"ld_st{k}") for k in range(2)]
        pad_ready, pad_written = sem("pad_ready"), sem("pad_written")
        setup_act, setup_dve, setup_pool = sem("setup_act"), sem("setup_dve"), sem("setup_pool")
        ln1_stat, ln1_rstd = sem("ln1_stat"), sem("ln1_rstd")
        b2_done, converted = sem("b2_done"), sem("converted")
        xh_ready, xhT_ps, xhT_ready = sem("xh_ready"), sem("xhT_ps"), sem("xhT_ready")
        qk_ps, qk_ready, v_ps, v_ready = sem("qk_ps"), sem("qk_ready"), sem("v_ps"), sem("v_ready")
        d_ready, pb_ready, xb_ready = sem("d_ready"), sem("pb_ready"), sem("xb_ready")
        s_ps, biased, scored, probs = sem("s_ps"), sem("biased"), sem("scored"), sem("probs")
        pt_ps, pt_hi, pt_lo, pv = sem("pt_ps"), sem("pt_hi"), sem("pt_lo"), sem("pv")
        o_ready, oT_ps, oT_ready, y_ps, x1_ready = (sem("o_ready"), sem("oT_ps"), sem("oT_ready"),
                                                    sem("y_ps"), sem("x1_ready"))
        dve_own, pool_own, act_own = sem("dve_own"), sem("pool_own"), sem("act_own")
        ln2_stat, ln2_rstd = sem("ln2_stat"), sem("ln2_rstd")
        xh2_ready, x2T_ps, x2_hi, x2_lo, gate_ps, gated = (sem("xh2_ready"), sem("x2T_ps"), sem("x2_hi"),
                                                         sem("x2_lo"), sem("gate_ps"), sem("gated"))
        wd_ready, we_ready, sel_ready, rank_ps, routed = (sem("wd_ready"), sem("we_ready"), sem("sel_ready"),
                                                        sem("rank_ps"), sem("routed"))
        pay_ready = sem("pay_ready")
        dispatched = [sem(f"dispatched{k}") for k in range(2)]
        su_ps, sg_ready, sh_ready, sd_used, sy_ps, acc_ready = (sem("su_ps"), sem("sg_ready"), sem("sh_ready"),
                                                              sem("sd_used"), sem("sy_ps"), sem("acc_ready"))
        out_written = sem("out_written")
        xs_in = [sem(f"xs_in{k}") for k in range(2)]
        xsT_ps, xs_hi, xs_lo, ids_ready = sem("xsT_ps"), sem("xs_hi"), sem("xs_lo"), sem("ids_ready")
        b1_ready, up_ps, g_ready, h_ready, down_ps, y_ready = (sem("b1_ready"), sem("up_ps"), sem("g_ready"),
                                                               sem("h_ready"), sem("down_ps"), sem("y_ready"))
        added = [sem(f"added{k}") for k in range(2)]
        dpos_done, dneg_done, conv_hi = sem("dpos_done"), sem("dneg_done"), sem("conv_hi")
        vh_done, rs_done, st_done, sh_hi, h_hi, acc_half = (sem("vh_done"), sem("rs_done"), sem("st_done"),
                                                          sem("sh_hi"), sem("h_hi"), sem("acc_half"))

        def pairs(eng, body):
            body(0, 0)
            body(1, 1)
            with eng.Fori(1, PAIRS - 1) as i:
                body(2 * i, 0)
                body(2 * i + 1, 1)
            body(B - 2, 0)
            body(B - 1, 1)

        passed = {}

        def wait_alone(eng, name, s, value):
            if name not in passed:
                passed[name] = sem(f"passed_{name}")
            eng.wait_ge(s, value)
            eng.sem_inc(passed[name], 1)

        def tiles(eng, body):
            body(0, 0, True)
            body(1, 1, True)
            with eng.Fori(1, SLOTS // 2) as i:
                body(2 * i, 0, True)
                body(2 * i + 1, 1, True)
            body(SLOTS - 1, 0, False)

        def first(b, n=1):
            return isinstance(b, int) and b < n

        def last(b):
            return isinstance(b, int) and b == B - 1

        block = ctx.enter_context(nc.Block())

        @block.sync
        def _(sp):
            sp.dma_start(cst[:], consts).then_inc(ld_par, 16)
            sp.dma_start(col[:], cols).then_inc(ld_par, 16)
            sp.dma_start(row[:], rows.to_broadcast([P, V_N])).then_inc(ld_par, 16)
            for k in range(4):
                sp.dma_start(xres[:, k * 4 * D:(k + 1) * 4 * D].rearrange("p (b d) -> p b d", d=D),
                             x[4 * k:4 * k + 4].rearrange("b p d -> p b d")).then_inc(ld_x[k], 16)
            sp.dma_start(wp.rearrange("p (k d) -> p k d", d=D), wproj.rearrange("k (c p) d -> p (k c) d", p=P)).then_inc(ld_wp, 16)

            def load_seq(b, par):
                if not first(b, 2):
                    sp.wait_ge(v_ps, b - 1)
                    sp.wait_ge(d_ready, b - 1)
                sp.dma_start(cT[par].rearrange("p (c t) -> p c t", c=DC),
                             ctxT[:, :, bass.ds(b * T, T)].rearrange("c p t -> p c t")).then_inc(ld_ctx[par], 16)
                sp.dma_start(fr[par], frac[:, bass.ds(b * T, T)].to_broadcast([P, T])).then_inc(ld_ctx[par], 16)

            load_seq(0, 0)
            load_seq(1, 1)
            sp.dma_start(stage[:], b2.to_broadcast([P, E * D])).then_inc(ld_b2, 16)
            sp.wait_ge(pad_ready, 1)
            sp.dma_start(xs_dram.rearrange("(j p) d -> p j d", p=P),
                         padt.rearrange("p (o d) -> p o d", o=1).to_broadcast([P, SLOTS, ROW])).then_inc(pad_written, 16)
            sp.dma_start(out[N:N + P, :], padt[:, 0:D]).then_inc(pad_written, 16)

            def load_weights(s, half):
                for k in range(2):
                    if not (isinstance(s, int) and s == 0 and half == 0):
                        sp.wait_ge(converted, 4 * s + 2 * half + k - 1)
                    if half == 0:
                        sp.dma_start(stage[:, k * HID:(k + 1) * HID],
                                     w1[bass.ds(s * D + k * P, P), :]).then_inc(ld_st[k], 16)
                    else:
                        sp.dma_start(stage[:, k * HID:(k + 1) * HID].rearrange("p (c d) -> p c d", d=D),
                                     w2[bass.ds(s * HID + k * 4 * P, 4 * P), :]
                                     .rearrange("(c p) d -> p c d", p=P)).then_inc(ld_st[k], 16)

            sp.wait_ge(b2_done, 1)
            load_weights(0, 0)
            load_weights(0, 1)
            with sp.Fori(1, EARLY) as i:
                load_seq(2 * i, 0)
                load_seq(2 * i + 1, 1)
                load_weights(i, 0)
                load_weights(i, 1)
            with sp.Fori(EARLY, PAIRS) as i:
                load_seq(2 * i, 0)
                load_seq(2 * i + 1, 1)
            with sp.Fori(EARLY, 1 + E) as s:
                load_weights(s, 0)
                load_weights(s, 1)

            with sp.Fori(0, GROUPS) as g:
                sp.wait_ge(acc_ready, 4 * g + 4)
                sp.dma_start(out[bass.ds(g * 512, 512), :].rearrange("(t p) d -> p t d", p=P),
                             xres[:, bass.ds(g * 4 * D, 4 * D)].rearrange("p (t d) -> p t d", d=D)).then_inc(out_written, 16)

            for k in range(2):
                sp.wait_ge(dispatched[k], 16 * TOPK * B // 2)
            sp.wait_ge(converted, 4 * (1 + E))

            def load_tile(j, par):
                if not first(j, 2):
                    sp.wait_ge(xsT_ps, j - 1)
                    sp.wait_ge(ids_ready, j - 1)
                sp.dma_start(xs[par], xs_dram[bass.ds(j * P, P), :]).then_inc(xs_in[par], 16)

            load_tile(0, 0)
            load_tile(1, 1)
            with sp.Fori(1, SLOTS // 2) as i:
                load_tile(2 * i, 0)
                load_tile(2 * i + 1, 1)
            load_tile(SLOTS - 1, 0)

        @block.gpsimd
        def _(pool):
            own = [0]

            def link(ins):
                own[0] += 1
                ins.then_inc(pool_own, 1)
                pool.wait_ge(pool_own, own[0])

            link(nc.gpsimd.memset(mhalf[:], -0.5))
            nc.gpsimd.memset(padt, 0.0).then_inc(pool_own, 1)
            own[0] += 1
            pool.wait_ge(pool_own, own[0])
            pool.wait_ge(ld_par, 48)
            nc.gpsimd.tensor_copy(padt[:, D + 1:D + 2], cst[:, C_PAD:C_PAD + 1]).then_inc(pad_ready, 1)
            pool.wait_ge(setup_act, 2)
            link(nc.gpsimd.tensor_scalar(bo_t, row[:, V_BO:V_BO + D], tgx[:, 0:1], None, ALU.mult))
            nc.gpsimd.tensor_scalar(bs2t, row[:, V_BS2:V_BS2 + D], tgf[:, 0:1], None, ALU.mult).then_inc(setup_pool, 1)
            pool.wait_ge(ln1_stat, B)
            link(nc.gpsimd.tensor_scalar(rstd1[:], mv1[:, :, 1], EPS, None, ALU.add))
            nc.gpsimd.tensor_tensor(rstd1[:], rstd1[:], mhalf[:], ALU.pow).then_inc(ln1_rstd, 1)
            pool.wait_ge(setup_dve, 1)

            def seq(b, par):
                i = b // 2 if isinstance(b, int) else None
                if isinstance(b, int):
                    pool.wait_ge(ld_ctx[par], 32 * (i + 1))
                else:
                    pool.wait_ge(ld_ctx[par], 16 * (b - par) + 32)
                if not first(b):
                    pool.wait_ge(pb_ready, R * b)
                nc.gpsimd.tensor_tensor(dd, fr[par], col[:, bass.ds(K_FR + b, 1)].to_broadcast([P, T]), ALU.subtract).then_inc(d_ready, 1)
                wait_alone(pool, "pool", d_ready, b + 1)
                nc.gpsimd.tensor_scalar(dpos, dd, 0.0, CLAMP, ALU.max, ALU.min).then_inc(dpos_done, 1)
                if not first(b, 2):
                    wait_alone(pool, "pool", biased, R * (b - 1))
                nc.gpsimd.tensor_scalar(dneg[par], dd, 0.0, -CLAMP, ALU.min, ALU.max).then_inc(dneg_done, 1)
                wait_alone(pool, "pool", dpos_done, b + 1)
                for r in range(R):
                    if not first(b):
                        wait_alone(pool, "pool", scored, R * b + r - 3)
                    for j in range(HR):
                        h = head(r, j)
                        ins = nc.gpsimd.tensor_scalar(pb[r][:, j * T:(j + 1) * T], dpos, apd[:, h:h + 1], None, ALU.mult)
                    ins.then_inc(pb_ready, 1)
                pool.wait_ge(xh_ready, b + 1)
                xb = xres[:, bass.ds(b * D, D)]
                nc.gpsimd.tensor_tensor(xb, xb, bo_t, ALU.add).then_inc(xb_ready, 1)

            def convert(s, half):
                for k in range(2):
                    base = s * WS + (W2H if half else W1H) + k * HID
                    hi = W[:, bass.ds(base, HID)]
                    lo = W[:, bass.ds(base + DC * HID, HID)]
                    src = stage[:, k * HID:(k + 1) * HID]
                    pool.wait_ge(ld_st[k], 32 * s + 16 * half + 16)
                    nc.gpsimd.tensor_copy(hi, src).then_inc(conv_hi, 1)
                    pool.wait_ge(conv_hi, 4 * s + 2 * half + k + 1)
                    nc.gpsimd.tensor_tensor(lo, src, hi, ALU.subtract).then_inc(converted, 1)

            def both(b, par, s=None):
                seq(b, par)
                if s is not None:
                    convert(s, par)

            for par in range(2):
                both(par, par, 0)
            with pool.Fori(1, EARLY) as i:
                for par in range(2):
                    both(2 * i + par, par, i)
            with pool.Fori(EARLY, PAIRS) as i:
                for par in range(2):
                    both(2 * i + par, par)

            pool.wait_ge(ln2_stat, B)
            own[0] += 1
            nc.gpsimd.tensor_scalar(rstd2[:], mv2[:, :, 1], EPS, None, ALU.add).then_inc(pool_own, 1)
            pool.wait_ge(pool_own, own[0])
            nc.gpsimd.tensor_tensor(rstd2[:], rstd2[:], mhalf[:], ALU.pow).then_inc(ln2_rstd, 1)

            pool.wait_ge(x1_ready, B)
            with pool.Fori(EARLY, 1 + E) as s:
                convert(s, 0)
                convert(s, 1)

            pool.wait_ge(pad_written, 32)
            with pool.Fori(0, PAIRS) as i:
                for par in range(2):
                    b = 2 * i + par
                    wait_alone(pool, "pool", pay_ready, b + 1)
                    for k in range(TOPK):
                        nc.gpsimd.indirect_dma_start(
                            xs_dram, bass.IndirectOffsetOnAxis(place[:, par, k:k + 1], axis=0),
                            pay[:, par, k, :], None).then_inc(dispatched[par], 16)

            pool.wait_ge(out_written, 16 * GROUPS)

            def add_tile(j, par):
                pool.wait_ge(y_ready, j + 1)
                pool.wait_ge(ids_ready, j + 1)
                if not first(j):
                    wait_alone(pool, "pool", added[1 - par], 16 * ((j + 1) // 2) if isinstance(j, int) else 8 * (j + par))
                nc.gpsimd.indirect_dma_start(
                    out, bass.IndirectOffsetOnAxis(idu[:, par, :], axis=0),
                    ysb[par], None, compute_op=ALU.add).then_inc(added[par], 16)

            add_tile(0, 0)
            add_tile(1, 1)
            with pool.Fori(1, SLOTS // 2) as i:
                add_tile(2 * i, 0)
                add_tile(2 * i + 1, 1)
            add_tile(SLOTS - 1, 0)
            pool.wait_ge(added[0], 16 * (SLOTS // 2 + 1))
            pool.wait_ge(added[1], 16 * (SLOTS // 2))


        @block.scalar
        def _(act):
            act.wait_ge(ld_par, 48)
            nc.scalar.activation(tgx[:], row[:, V_GX:V_GX + 1], ACT.Tanh).then_inc(setup_act, 1)
            nc.scalar.activation(tgf[:], row[:, V_GF:V_GF + 1], ACT.Tanh).then_inc(setup_act, 1)
            act.wait_ge(setup_dve, 1)

            def move_xhT(b):
                act.wait_ge(xhT_ps, b + 1)
                if not first(b):
                    act.wait_ge(v_ps, b)
                nc.scalar.activation(xhT, psM[:, 0:DC * T], ACT.Copy).then_inc(xhT_ready, 1)

            def move_q(b, par):
                act.wait_ge(qk_ps, b + 1)
                if not first(b, 2):
                    act.wait_ge(s_ps, R * (b - 1))
                for c in range(DC):
                    nc.scalar.activation(qT[par][:, c * T:(c + 1) * T], psQK[:, c * T:(c + 1) * T], ACT.Identity,
                                         scale=gs[:, 0:1], bias=bqs[:, c:c + 1])

            def move_k(b, par):
                for e in range(2):
                    for c in range(DC):
                        ins = nc.scalar.activation(
                            kz[par][:, (e * DC + c) * T:(e * DC + c + 1) * T],
                            psQK[:, (DC + c) * T:(DC + c + 1) * T], ACT.Identity,
                            scale=cst[:, C_EVEN + e:C_EVEN + e + 1], bias=bkm[:, e, c:c + 1])
                ins.then_inc(qk_ready, 1)

            def high(n, k, wait_free):
                act.wait_ge(pt_ps, n + 1)
                if wait_free:
                    act.wait_ge(pv, n - 1)
                nc.scalar.activation(pth[k], psT[k][:], ACT.Copy).then_inc(pt_hi, 1)

            def exps(n, r, par):
                act.wait_ge(scored, n + 1)
                for j in range(HR):
                    q = r * HR + j
                    ins = nc.scalar.activation(sc[r][:, j * T:(j + 1) * T], sc[r][:, j * T:(j + 1) * T], ACT.Exp,
                                               scale=-1.0, bias=mn[:, par, q:q + 1], accum_out=sm[:, par, q:q + 1])
                ins.then_inc(probs, 1)

            def move_oT(b):
                act.wait_ge(oT_ps, b + 1)
                if not first(b):
                    act.wait_ge(y_ps, b)
                for c in range(DC):
                    ins = nc.scalar.activation(oT[:, c * T:(c + 1) * T], psM[:, c * T:(c + 1) * T], ACT.Identity,
                                               bias=col[:, K_BV + c:K_BV + c + 1])
                ins.then_inc(oT_ready, 1)

            def seq(b, par):
                for r in range(R):
                    n = R * b + r
                    if not (first(b) and r == 0):
                        high(n - 1, (r - 1) % 2, not (first(b) and r < 3))
                    if r == 3 and not first(b):
                        move_oT(b - 1)
                    if r == 0 and not first(b, 2):
                        act.wait_ge(o_ready, b - 1)
                    exps(n, r, par)
                    if not last(b):
                        if r == 0:
                            move_xhT(b + 1)
                        if r == 1:
                            move_q(b + 1, 1 - par)
                        if r == 2:
                            move_k(b + 1, 1 - par)

            move_xhT(0)
            move_q(0, 0)
            move_k(0, 0)
            pairs(act, seq)
            high(STEPS - 1, 1, True)
            move_oT(B - 1)

            def high2(b, par):
                act.wait_ge(x2T_ps, b + 1)
                nc.scalar.activation(xT2[:, 0:DC * N].rearrange("p (c n) -> p c n", c=DC)[:, :, bass.ds(b * T, T)],
                                     bank[6 + par][:, 0:DC * T].rearrange("p (c t) -> p c t", c=DC), ACT.Copy).then_inc(x2_hi, 1)

            with act.Fori(0, PAIRS) as i:
                high2(2 * i, 0)
                high2(2 * i + 1, 1)
            act.wait_ge(wd_ready, 1)
            nc.scalar.activation(ed[:], ed[:], ACT.Exp).then_inc(we_ready, 1)

            def gelu_shared(g):
                for c in range(HC):
                    act.wait_ge(su_ps, HC * g + c + 1)
                    if not (first(g) and c < 2):
                        act.wait_ge(sh_ready, HC * g + c - 1)
                    nc.scalar.activation(hbuf[:, c % 2, :], bank[c % 2][:], ACT.Gelu,
                                         bias=col[:, K_BS1 + c:K_BS1 + c + 1]).then_inc(sg_ready, 1)

            gelu_shared(0)
            with act.Fori(1, GROUPS) as g:
                gelu_shared(g)

            def high_tile(j, par):
                act.wait_ge(xsT_ps, j + 1)
                if not first(j, 2):
                    act.wait_ge(up_ps, 2 * (j - 1))
                nc.scalar.activation(xsT[par][:, 0:DC * P], bank[6 + par][:, 0:DC * P], ACT.Copy).then_inc(xs_hi, 1)

            def gelu_tile(j, par):
                act.wait_ge(b1_ready, j + 1)
                for half in range(2):
                    act.wait_ge(up_ps, 2 * j + half + 1)
                    if not first(j):
                        act.wait_ge(h_ready, 2 * (j - 1) + half + 1)
                    for c in range(4):
                        ins = nc.scalar.activation(hbuf[:, half, c * P:(c + 1) * P],
                                                   bank[2 * par + half][:, c * P:(c + 1) * P], ACT.Gelu,
                                                   bias=b1t[:, par, 4 * half + c:4 * half + c + 1])
                    ins.then_inc(g_ready, 1)

            high_tile(0, 0)
            tiles(act, lambda j, par, more: (more and high_tile(j + 1, 1 - par), gelu_tile(j, par)))

        @block.vector
        def _(dve):
            own = [0]

            def link(ins):
                own[0] += 1
                ins.then_inc(dve_own, 1)
                dve.wait_ge(dve_own, own[0])

            dve.wait_ge(ld_par, 48)
            link(nc.vector.tensor_scalar(gs[:], row[:, V_GAMMA:V_GAMMA + 1], -(HD ** -0.5), None, ALU.mult))
            link(nc.vector.tensor_scalar(bqs[:], col[:, K_BQ:K_BQ + DC], gs[:, 0:1], None, ALU.mult))
            for e in range(2):
                link(nc.vector.tensor_scalar(bkm[:, e, :], col[:, K_BK:K_BK + DC], cst[:, C_EVEN + e:C_EVEN + e + 1], None, ALU.mult))
            link(nc.vector.tensor_scalar(apd[:], row[:, V_AP:V_AP + H], row[:, V_DELTA:V_DELTA + 1], -1.0, ALU.mult, ALU.mult))
            link(nc.vector.tensor_scalar(and_[:], row[:, V_AN:V_AN + H], row[:, V_DELTA:V_DELTA + 1], -1.0, ALU.mult, ALU.mult))
            gw = col[:, K_GW:K_GW + DC * E].rearrange("p (c e) -> p c e", c=DC)
            link(nc.vector.tensor_copy(gwhl[:, 0], gw))
            link(nc.vector.tensor_tensor(gwhl[:, 1], gw, gwhl[:, 0], ALU.subtract))
            link(nc.vector.tensor_copy(upb[:], cst[:, C_UP:C_UP + P]))
            link(nc.vector.memset(oneb[:], 1.0))
            nc.vector.tensor_copy(selb[:], cst[:, C_R01:C_R01 + 1].to_broadcast([P, P])).then_inc(setup_dve, 1)
            for b in range(B):
                if b % 4 == 0:
                    dve.wait_ge(ld_x[b // 4], 16)
                link(nc.vector.bn_stats(st6[:, b, :], xres[:, b * D:(b + 1) * D]))
                nc.vector.bn_aggr(mv1[:, b, :], st6[:, b, :]).then_inc(ln1_stat, 1)

            def norm1(b):
                if first(b):
                    dve.wait_ge(ln1_rstd, 1)
                else:
                    dve.wait_ge(xhT_ps, b)
                nc.vector.tensor_scalar(xh, xres[:, bass.ds(b * D, D)], mv1[:, bass.ds(b, 1), 0], rstd1[:, bass.ds(b, 1)],
                                        ALU.subtract, ALU.mult).then_inc(xh_ready, 1)

            def values(b, par):
                dve.wait_ge(v_ps, b + 1)
                if not first(b, 2):
                    dve.wait_ge(pv, R * (b - 1))
                nc.vector.tensor_copy(vh[par], psVY[:, 0:D]).then_inc(vh_done, 1)
                dve.wait_ge(vh_done, b + 1)
                nc.vector.tensor_tensor(vl[par], psVY[:, 0:D], vh[par], ALU.subtract).then_inc(v_ready, 1)

            def bias(n, r, par, b):
                dve.wait_ge(s_ps, n + 1)
                if r == 0:
                    dve.wait_ge(dneg_done, b + 1)
                if not first(b):
                    dve.wait_ge(pt_ps, n - 3)
                for j in range(HR):
                    h = head(r, j)
                    ins = nc.vector.scalar_tensor_tensor(sc[r][:, j * T:(j + 1) * T], dneg[par], and_[:, h:h + 1],
                                                         psS[r % 2][:, j * T:(j + 1) * T], ALU.mult, ALU.add)
                ins.then_inc(biased, 1)

            def low(n, k, wait_free):
                dve.wait_ge(pt_hi, n + 1)
                if wait_free:
                    dve.wait_ge(pv, n - 1)
                nc.vector.tensor_tensor(ptl[k], psT[k][:], pth[k], ALU.subtract).then_inc(pt_lo, 1)

            def least(n, r, par, b):
                dve.wait_ge(pb_ready, n + 1)
                if not first(b, 2):
                    dve.wait_ge(probs, n - 7)
                wait_alone(dve, "dve", biased, n + 1)
                for j in range(HR):
                    s = sc[r][:, j * T:(j + 1) * T]
                    q = r * HR + j
                    ins = nc.vector.tensor_tensor_reduce(out=s, in0=s, in1=pb[r][:, j * T:(j + 1) * T], scale=1.0,
                                                         scalar=3.0e38, op0=ALU.add, op1=ALU.min, accum_out=mn[:, par, q:q + 1])
                ins.then_inc(scored, 1)

            def output(b, par):
                dve.wait_ge(pv, R * b + R)
                if not first(b):
                    dve.wait_ge(oT_ps, b)
                nc.vector.reciprocal(rs[:], sm[:, par, :]).then_inc(rs_done, 1)
                dve.wait_ge(rs_done, b + 1)
                for c in range(DC):
                    ins = nc.vector.tensor_tensor(
                        on[:, c * P:(c + 1) * P].rearrange("p (r e d) -> p r e d", r=R, e=2),
                        psO[:, c * P:(c + 1) * P].rearrange("p (r e d) -> p r e d", r=R, e=2),
                        rs[:].rearrange("p (r c e o) -> p c r e o", r=R, c=DC, o=1)[:, c].to_broadcast([P, R, 2, HD]),
                        ALU.mult)
                ins.then_inc(o_ready, 1)

            def residual(b):
                dve.wait_ge(y_ps, b + 1)
                dve.wait_ge(xb_ready, b + 1)
                xb = xres[:, bass.ds(b * D, D)]
                nc.vector.scalar_tensor_tensor(xb, psVY[:, D:2 * D], tgx[:, 0:1], xb, ALU.mult, ALU.add).then_inc(x1_ready, 1)
                wait_alone(dve, "dve", x1_ready, b + 1)
                nc.vector.bn_stats(st6[:, bass.ds(b, 1), :].rearrange("p b k -> p (b k)"), xb).then_inc(st_done, 1)

            def seq(b, par):
                if not last(b):
                    norm1(b + 1)
                for r in range(R):
                    n = R * b + r
                    bias(n, r, par, b)
                    if r == 1 and not first(b):
                        output(b - 1, 1 - par)
                    if r == 2 and not last(b):
                        values(b + 1, 1 - par)
                    if not (first(b) and r == 0):
                        low(n - 1, (r - 1) % 2, not (first(b) and r < 3))
                    least(n, r, par, b)
                    if r == 3 and not first(b):
                        residual(b - 1)

            norm1(0)
            values(0, 0)
            dve.wait_ge(ld_b2, 16)
            link(nc.vector.tensor_copy(b2hl[:], stage[:]))
            link(nc.vector.tensor_tensor(stage[:], stage[:], b2hl[:], ALU.subtract))
            link(nc.vector.tensor_scalar(b2hl[:], b2hl[:], cst[:, C_R0:C_R0 + 1], None, ALU.mult))
            nc.vector.scalar_tensor_tensor(b2hl[:], stage[:], cst[:, C_R1:C_R1 + 1], b2hl[:], ALU.mult, ALU.add).then_inc(b2_done, 1)
            pairs(dve, seq)
            low(STEPS - 1, 1, True)
            output(B - 1, 1)
            residual(B - 1)
            dve.wait_ge(st_done, B)
            for b in range(B):
                nc.vector.bn_aggr(mv2[:, b, :], st6[:, b, :]).then_inc(ln2_stat, 1)

            dve.wait_ge(ln2_rstd, 1)

            def norm2(b, par):
                dve.wait_ge(x2T_ps, b - 1) if not first(b, 2) else None
                nc.vector.tensor_scalar(hbuf[:, par, 0:D], xres[:, bass.ds(b * D, D)], mv2[:, bass.ds(b, 1), 0],
                                        rstd2[:, bass.ds(b, 1)], ALU.subtract, ALU.mult).then_inc(xh2_ready, 1)

            def low2(b, par):
                dve.wait_ge(x2_hi, b + 1)
                xT = xT2[:, :].rearrange("p (k c n) -> p k c n", k=2, c=DC)
                nc.vector.tensor_tensor(xT[:, 1, :, bass.ds(b * T, T)],
                                        bank[6 + par][:, 0:DC * T].rearrange("p (c t) -> p c t", c=DC),
                                        xT[:, 0, :, bass.ds(b * T, T)], ALU.subtract).then_inc(x2_lo, 1)

            norm2(0, 0)
            norm2(1, 1)
            with dve.Fori(1, PAIRS) as i:
                for par in range(2):
                    low2(2 * i + par - 2, par)
                    norm2(2 * i + par, par)
            low2(B - 2, 0)
            low2(B - 1, 1)

            dve.wait_ge(gate_ps, 1)
            link(nc.vector.tensor_tensor(lg, bank[4][:, 0:B * E].rearrange("p (b e) -> p b e", e=E),
                                         row[:, V_GB:V_GB + E].rearrange("p (o e) -> p o e", o=1).to_broadcast([P, B, E]), ALU.add))
            for b in range(B):
                ins = nc.vector.max(mx8[:, b, :], lg[:, b, :])
            link(ins)
            for b in range(B):
                ins = nc.vector.max_index(ix8[:, b, :], mx8[:, b, :], lg[:, b, :])
            link(ins)
            nc.vector.tensor_tensor(ed[:], mx8[:, :, 1], mx8[:, :, 0], ALU.subtract).then_inc(wd_ready, 1)
            link(nc.vector.tensor_copy(ixf[:], ix8[:, :, 0:TOPK]))
            iota = cst[:, C_IOTA:C_IOTA + E].rearrange("p (o e) -> p o e", o=1).to_broadcast([P, B, E])
            for k in range(TOPK):
                link(nc.vector.tensor_tensor(oh[k], iota, ixf[:, :, k:k + 1].to_broadcast([P, B, E]), ALU.is_equal))
            nc.vector.tensor_tensor(selm, oh[0], oh[1], ALU.add).then_inc(sel_ready, 1)
            dve.wait_ge(we_ready, 1)
            link(nc.vector.tensor_scalar(wt[:, :, 1], ed[:], 1.0, None, ALU.add))
            link(nc.vector.reciprocal(wt[:, :, 0], wt[:, :, 1]))
            link(nc.vector.tensor_tensor(wt[:, :, 1], ed[:], wt[:, :, 0], ALU.mult))
            link(nc.vector.tensor_scalar(wid[:, :, :, 0], wt[:], tgf[:, 0:1], None, ALU.mult))
            for k in range(TOPK):
                link(nc.vector.tensor_copy(wid[:, :, k, 1], cst[:, C_TOK:C_TOK + B]))
            dve.wait_ge(rank_ps, 1)
            cnt = bank[5][:, B * E:2 * B * E].rearrange("p (b e) -> p b e", e=E)
            link(nc.vector.tensor_copy(ca[0], cnt))
            a = 0
            step = 1
            while step < B:
                link(nc.vector.tensor_copy(ca[1 - a][:, 0:step, :], ca[a][:, 0:step, :]))
                link(nc.vector.tensor_tensor(ca[1 - a][:, step:B, :], ca[a][:, step:B, :], ca[a][:, 0:B - step, :], ALU.add))
                a, step = 1 - a, 2 * step
            link(nc.vector.tensor_tensor(offs, ca[a], cnt, ALU.subtract))
            link(nc.vector.tensor_scalar(te_i[:], ca[a][:, B - 1, :], float(P - 1), None, ALU.add))
            link(nc.vector.tensor_single_scalar(te_i[:], te_i[:], 7, op=ALU.arith_shift_right))
            link(nc.vector.tensor_copy(te[0][:], te_i[:]))
            link(nc.vector.tensor_copy(te[1][:], te[0][:]))
            k, step = 1, 1
            while step < E:
                link(nc.vector.tensor_copy(te[3 - k][:, 0:step], te[k][:, 0:step]))
                link(nc.vector.tensor_tensor(te[3 - k][:, step:E], te[k][:, step:E], te[k][:, 0:E - step], ALU.add))
                k, step = 3 - k, 2 * step
            ends, base = te[k], te[3 - k]
            link(nc.vector.tensor_tensor(
                tcmp, cst[:, C_TILE:C_TILE + SLOTS].rearrange("p (j o) -> p j o", o=1).to_broadcast([P, SLOTS, E]),
                ends[:].rearrange("p (o e) -> p o e", o=1).to_broadcast([P, SLOTS, E]), ALU.is_ge))
            link(nc.vector.tensor_reduce(tef[:], tcmp, AX.X, ALU.add))
            link(nc.vector.tensor_scalar(tei[:], tef[:], float(E - 1), None, ALU.min))
            link(nc.vector.tensor_tensor(base[:], ends[:], te[0][:], ALU.subtract))
            link(nc.vector.tensor_scalar(base[:], base[:], float(P), None, ALU.mult))
            link(nc.vector.tensor_tensor(offs, offs, bank[5][:, 0:B * E].rearrange("p (b e) -> p b e", e=E), ALU.add))
            link(nc.vector.tensor_tensor(offs, offs, base[:].rearrange("p (o e) -> p o e", o=1).to_broadcast([P, B, E]), ALU.add))
            for k in range(TOPK):
                link(nc.vector.tensor_tensor(ca[0], offs, oh[k], ALU.mult))
                link(nc.vector.tensor_reduce(posf[:, k, :], ca[0], AX.X, ALU.add))
            nc.vector.tensor_copy(posu[:], posf[:]).then_inc(routed, 1)
            dve.wait_ge(routed, 1)
            dve.wait_ge(pad_written, 32)

            def payload(b, par, k, m):
                if k == 0:
                    nc.vector.tensor_copy(place[:, par, :], posu[:, :, bass.ds(b, 1)].rearrange("p k b -> p (k b)"))
                nc.vector.tensor_scalar(pay[:, par, k, 0:D], xres[:, bass.ds(b * D, D)], mv2[:, bass.ds(b, 1), 0],
                                        rstd2[:, bass.ds(b, 1)], ALU.subtract, ALU.mult)
                ins = nc.vector.tensor_copy(pay[:, par, k, D:ROW], wid[:, bass.ds(b, 1), k, :].rearrange("p b k -> p (b k)"))
                if k == 1:
                    ins.then_inc(pay_ready, 1)

            def shared_group(g, y):
                for c in range(HC):
                    m = HC * g + c
                    dve.wait_ge(sg_ready, m + 1)
                    if not (first(g) and c < 2):
                        dve.wait_ge(sd_used, m - 1)
                    nc.vector.tensor_copy(hsplit[:, c % 2, 0, :], hbuf[:, c % 2, :]).then_inc(sh_hi, 1)
                    dve.wait_ge(sh_hi, m + 1)
                    nc.vector.tensor_tensor(hsplit[:, c % 2, 1, :], hbuf[:, c % 2, :], hsplit[:, c % 2, 0, :],
                                            ALU.subtract).then_inc(sh_ready, 1)
                    b, k = 4 * g + c // 2, c % 2
                    par = (c // 2) % 2
                    if k == 0 and not (first(g) and c < 4):
                        dve.wait_ge(dispatched[par], 16 * (4 * g + c // 2 - par))
                    payload(b, par, k, m)
                dve.wait_ge(sy_ps, g + 1)
                for t in range(4):
                    xb = xres[:, bass.ds((4 * g + t) * D, D)]
                    nc.vector.scalar_tensor_tensor(xb, bank[2 + 2 * y + t // 2][:, (t % 2) * D:(t % 2 + 1) * D], tgf[:, 0:1], xb,
                                                   ALU.mult, ALU.add).then_inc(acc_half, 1)
                dve.wait_ge(acc_half, 4 * g + 4)
                dve.wait_ge(setup_pool, 1)
                for t in range(4):
                    xb = xres[:, bass.ds((4 * g + t) * D, D)]
                    nc.vector.tensor_tensor(xb, xb, bs2t, ALU.add).then_inc(acc_ready, 1)

            shared_group(0, 0)
            shared_group(1, 1)
            with dve.Fori(1, GROUPS // 2) as i:
                shared_group(2 * i, 0)
                shared_group(2 * i + 1, 1)

            def low_tile(j, par):
                e = dve.value_load(tei[0:1, bass.ds(j, 1)], min_val=0, max_val=E - 1)
                if not first(j, 2):
                    dve.wait_ge(g_ready, 2 * (j - 1))
                    dve.wait_ge(added[par], 16 * ((j - 1 + 1) // 2) if isinstance(j, int) else 8 * (j - par))
                nc.vector.tensor_copy(b1t[:, par, :], col[:, bass.ds(K_B1 + e * HC, HC)]).then_inc(b1_ready, 1)
                dve.wait_ge(xs_in[par], 16 * (j // 2) + 16 if isinstance(j, int) else 8 * (j - par) + 16)
                nc.vector.tensor_copy(wx[:, par, :], xs[par][:, D:D + 1])
                nc.vector.tensor_copy(idu[:, par, :], xs[par][:, D + 1:D + 2]).then_inc(ids_ready, 1)
                dve.wait_ge(xs_hi, j + 1)
                if not first(j, 2):
                    dve.wait_ge(up_ps, 2 * (j - 1))
                nc.vector.tensor_tensor(xsT[par][:, DC * P:2 * DC * P], bank[6 + par][:, 0:DC * P], xsT[par][:, 0:DC * P],
                                        ALU.subtract).then_inc(xs_lo, 1)

            def split_tile(j, par):
                for half in range(2):
                    dve.wait_ge(g_ready, 2 * j + half + 1)
                    if half == 0 and not first(j, 2):
                        dve.wait_ge(down_ps, j - 1)
                    hi = hs[par][:, half * 512:(half + 1) * 512]
                    lo = hs[par][:, HID + half * 512:HID + (half + 1) * 512]
                    nc.vector.tensor_copy(hi, hbuf[:, half, :]).then_inc(h_hi, 1)
                    dve.wait_ge(h_hi, 2 * j + half + 1)
                    nc.vector.tensor_tensor(lo, hbuf[:, half, :], hi, ALU.subtract).then_inc(h_ready, 1)

            def weigh(j, par):
                dve.wait_ge(down_ps, j + 1)
                if not first(j, 2):
                    dve.wait_ge(added[par], 16 * (j // 2) if isinstance(j, int) else 8 * (j - par))
                nc.vector.tensor_scalar(ysb[par], bank[4 + par][:, 0:D], wx[:, par, 0:1], None, ALU.mult).then_inc(y_ready, 1)

            low_tile(0, 0)

            def body(j, par, more):
                if not first(j):
                    weigh(j - 1, 1 - par)
                if more:
                    low_tile(j + 1, 1 - par)
                split_tile(j, par)

            tiles(dve, body)
            weigh(SLOTS - 1, (SLOTS - 1) % 2)

        @block.tensor
        def _(pe):
            def mm(o, a, b, start, stop, **kw):
                return nc.tensor.matmul(o, a, b, start=start, stop=stop, **kw)

            def turn_xh(b):
                pe.wait_ge(xh_ready, b + 1)
                if not first(b, 3):
                    pe.wait_ge(oT_ready, b - 2)
                for c in range(DC):
                    ins = nc.tensor.transpose(psM[:, c * T:(c + 1) * T], xh[:, c * P:(c + 1) * P], ident)
                ins.then_inc(xhT_ps, 1)

            def project(b, par):
                pe.wait_ge(xhT_ready, b + 1)
                pe.wait_ge(ld_ctx[par], 32 * (b // 2 + 1) if isinstance(b, int) else 16 * (b - par) + 32)
                if not first(b):
                    pe.wait_ge(qk_ready, b)
                for k, src in ((0, xhT), (1, cT[par])):
                    for o in range(DC):
                        for c in range(DC):
                            ins = mm(psQK[:, (k * DC + o) * T:(k * DC + o + 1) * T], wproj_at(k, c)[:, o * P:(o + 1) * P],
                                     src[:, c * T:(c + 1) * T], c == 0, c == DC - 1)
                ins.then_inc(qk_ps, 1)
                if not first(b, 3):
                    pe.wait_ge(x1_ready, b - 2)
                if not first(b):
                    pe.wait_ge(v_ready, b)
                for c in range(DC):
                    ins = mm(psVY[:, 0:D], cT[par][:, c * T:(c + 1) * T], wproj_at(2, c), c == 0, c == DC - 1)
                ins.then_inc(v_ps, 1)

            def scores(n, r, par, b):
                if r == 0:
                    pe.wait_ge(qk_ready, b + 1)
                if not (first(b) and r < 2):
                    pe.wait_ge(biased, n - 1)
                rows = slice(32 * r, 32 * r + 32)
                for j in range(HR):
                    c, e = j // 2, j % 2
                    ins = mm(psS[r % 2][:, j * T:(j + 1) * T], qT[par][rows, c * T:(c + 1) * T],
                             kz[par][rows, (e * DC + c) * T:(e * DC + c + 1) * T], True, True)
                ins.then_inc(s_ps, 1)

            def turn_probs(n, r, b):
                pe.wait_ge(probs, n + 1)
                if not (first(b) and r < 2):
                    pe.wait_ge(pt_lo, n - 1)
                for j in range(HR):
                    ins = nc.tensor.transpose(psT[r % 2][:, j * T:(j + 1) * T], sc[r][:, j * T:(j + 1) * T], ident)
                ins.then_inc(pt_ps, 1)

            def weigh_values(n, r, par, b):
                pe.wait_ge(pt_lo, n + 1)
                if r == 0:
                    pe.wait_ge(v_ready, b + 1)
                    if not first(b):
                        pe.wait_ge(o_ready, b)
                k = r % 2
                for j in range(HR):
                    h = head(r, j)
                    cols_ = slice(h * HD, (h + 1) * HD)
                    pj = slice(j * T, (j + 1) * T)
                    mm(psO[:, cols_], pth[k][:, pj], vh[par][:, cols_], True, False)
                    mm(psO[:, cols_], pth[k][:, pj], vl[par][:, cols_], False, False)
                    ins = mm(psO[:, cols_], ptl[k][:, pj], vh[par][:, cols_], False, True)
                ins.then_inc(pv, 1)

            def turn_o(b):
                pe.wait_ge(o_ready, b + 1)
                if not last(b):
                    pe.wait_ge(xhT_ready, b + 3) if not (isinstance(b, int) and b + 3 > B) else None
                for c in range(DC):
                    ins = nc.tensor.transpose(psM[:, c * T:(c + 1) * T], on[:, c * P:(c + 1) * P], ident)
                ins.then_inc(oT_ps, 1)

            def project_o(b):
                pe.wait_ge(oT_ready, b + 1)
                if not (isinstance(b, int) and b + 3 > B):
                    pe.wait_ge(v_ready, b + 3)
                for c in range(DC):
                    ins = mm(psVY[:, D:2 * D], oT[:, c * T:(c + 1) * T], wproj_at(3, c), c == 0, c == DC - 1)
                ins.then_inc(y_ps, 1)

            def seq(b, par):
                for r in range(R):
                    n = R * b + r
                    if r < R - 1:
                        scores(n + 1, r + 1, par, b)
                    elif not last(b):
                        scores(n + 1, 0, 1 - par, b + 1)
                    if r == 3 and not first(b):
                        project_o(b - 1)
                    if r == 1 and not last(b):
                        project(b + 1, 1 - par)
                    turn_probs(n, r, b)
                    if r >= 1:
                        weigh_values(n - 1, r - 1, par, b)
                    elif not first(b):
                        weigh_values(n - 1, R - 1, 1 - par, b - 1)
                    if r == 0 and not last(b):
                        turn_xh(b + 1)
                    if r == 2 and not first(b):
                        turn_o(b - 1)

            pe.wait_ge(ld_par, 48)
            turn_xh(0)
            pe.wait_ge(ld_wp, 16)
            project(0, 0)
            scores(0, 0, 0, 0)
            pairs(pe, seq)
            weigh_values(STEPS - 1, R - 1, 1, B - 1)
            turn_o(B - 1)
            project_o(B - 1)

            def turn2(b, par):
                pe.wait_ge(xh2_ready, b + 1)
                if not first(b, 2):
                    pe.wait_ge(x2_lo, b - 1)
                for c in range(DC):
                    ins = nc.tensor.transpose(bank[6 + par][:, c * T:(c + 1) * T], hbuf[:, par, c * P:(c + 1) * P], ident)
                ins.then_inc(x2T_ps, 1)

            pe.wait_ge(x1_ready, B)
            turn2(0, 0)
            turn2(1, 1)
            with pe.Fori(1, PAIRS) as i:
                turn2(2 * i, 0)
                turn2(2 * i + 1, 1)
            pe.wait_ge(x2_lo, B)
            for b in range(B):
                for c in range(DC):
                    for p in range(4):
                        xk = xT2[:, (p % 2) * DC * N + c * N + b * T:(p % 2) * DC * N + c * N + (b + 1) * T]
                        ins = mm(bank[4][:, b * E:(b + 1) * E], xk, gwhl[:, p // 2, c, :],
                                 c == 0 and p == 0, c == DC - 1 and p == 3)
            ins.then_inc(gate_ps, 1)
            pe.wait_ge(sel_ready, 1)
            sel = selm.rearrange("p b e -> p (b e)")
            mm(bank[5][:, 0:B * E], upb[:], sel, True, True)
            mm(bank[5][:, B * E:2 * B * E], oneb[:], sel, True, True).then_inc(rank_ps, 1)

            def w_up(base, part, c, j):
                return W[:, bass.ds(base + (W1L if part else W1H) + c * HID + j * P, P)]

            def w_down(base, part, j):
                return W[:, bass.ds(base + (W2L if part else W2H) + j * D, D)]

            def shared_up(g, j):
                if not (first(g) and j < 2):
                    pe.wait_ge(sg_ready, HC * g + j - 1)
                n = 0
                for wpart, xpart in ((0, 0), (1, 0), (0, 1)):
                    for c in range(DC):
                        ins = mm(bank[j % 2][:], w_up(0, wpart, c, j),
                                 xT2[:, bass.ds(xpart * DC * N + c * N + g * 512, 512)], n == 0, n == 5)
                        n += 1
                ins.then_inc(su_ps, 1)

            def shared_down(g, y, j):
                pe.wait_ge(sh_ready, HC * g + j + 1)
                if j == 0 and not first(g, 2):
                    pe.wait_ge(acc_half, 4 * (g - 1))
                n = 0
                for hpart, wpart in ((0, 0), (0, 1), (1, 0)):
                    for t in range(4):
                        ins = mm(bank[2 + 2 * y + t // 2][:, (t % 2) * D:(t % 2 + 1) * D],
                                 hsplit[:, j % 2, hpart, t * P:(t + 1) * P], w_down(0, wpart, j),
                                 j == 0 and n == 0 and t % 2 == 0, j == HC - 1 and n == 2, skip_group_check=True)
                    n += 1
                ins.then_inc(sd_used, 1)
                return ins

            pe.wait_ge(routed, 1)
            pe.wait_ge(converted, 4)

            def shared_group(g, y):
                shared_up(g, 0)
                for j in range(1, HC):
                    shared_up(g, j)
                    shared_down(g, y, j - 1)
                shared_down(g, y, HC - 1)
                nc.tensor.matmul(bank[7][:, 0:1], oneb[:], oneb[:, 0:1], start=True, stop=True).then_inc(sy_ps, 1)

            shared_group(0, 0)
            shared_group(1, 1)
            with pe.Fori(1, GROUPS // 2) as i:
                shared_group(2 * i, 0)
                shared_group(2 * i + 1, 1)

            def turn_tile(j, par):
                pe.wait_ge(xs_in[par], 16 * (j // 2) + 16 if isinstance(j, int) else 8 * (j - par) + 16)
                if not first(j, 2):
                    pe.wait_ge(xs_lo, j - 1)
                for c in range(DC):
                    ins = nc.tensor.transpose(bank[6 + par][:, c * P:(c + 1) * P], xs[par][:, c * P:(c + 1) * P], ident)
                ins.then_inc(xsT_ps, 1)

            def base_of(j):
                e = pe.value_load(tei[0:1, bass.ds(j, 1)], min_val=0, max_val=E - 1)
                return (e + 1) * WS

            def up_tile(j, par):
                base = base_of(j)
                pe.wait_ge(xs_lo, j + 1)
                for half in range(2):
                    if not first(j, 2):
                        pe.wait_ge(g_ready, 2 * (j - 2) + half + 1)
                    for q in range(4):
                        n = 0
                        for wpart, xpart in ((0, 0), (1, 0), (0, 1)):
                            for c in range(DC):
                                ins = mm(bank[2 * par + half][:, q * P:(q + 1) * P], w_up(base, wpart, c, 4 * half + q),
                                         xsT[par][:, (xpart * DC + c) * P:(xpart * DC + c + 1) * P], n == 0, n == 5)
                                n += 1
                    ins.then_inc(up_ps, 1)

            def down_tile(j, par):
                base = base_of(j)
                if not first(j, 2):
                    pe.wait_ge(y_ready, j - 1)
                y = bank[4 + par][:, 0:D]
                mm(y, selb[:], b2hl[:, bass.ds((base - WS) // (WS // D), D)], True, False)
                for c in range(HC):
                    if c % 4 == 0:
                        pe.wait_ge(h_ready, 2 * j + c // 4 + 1)
                    for hpart, wpart in ((0, 0), (0, 1), (1, 0)):
                        ins = mm(y, hs[par][:, hpart * HID + c * P:hpart * HID + (c + 1) * P], w_down(base, wpart, c),
                                 False, c == HC - 1 and hpart == 1)
                ins.then_inc(down_ps, 1)

            turn_tile(0, 0)

            def body(j, par, more):
                if more:
                    turn_tile(j + 1, 1 - par)
                up_tile(j, par)
                if not first(j):
                    down_tile(j - 1, 1 - par)

            pe.wait_ge(converted, 4 * (1 + E))
            pe.wait_ge(b2_done, 1)
            tiles(pe, body)
            down_tile(SLOTS - 1, (SLOTS - 1) % 2)


def kernel(**inputs):
    import numpy as np
    import concourse.bacc as bacc
    from concourse.bass_utils import run_bass_kernel_spmd

    def a(name):
        return np.asarray(inputs[name], order="C")

    def chunks(v):
        return v.reshape(-1, P).T

    f = np.float32
    x = a("x")
    ctxT = np.ascontiguousarray(a("ctx_1024").reshape(N, D).T.reshape(DC, P, N))
    frac = np.ascontiguousarray(a("fside_BxS2_0").reshape(1, N))
    wproj = np.stack([a(f"L0_xattn_W{k}").T for k in "qkvo"])
    p = np.arange(P)
    consts = np.concatenate([
        np.eye(P), p[:, None] < p[None, :],
        np.stack([p % 32 < HD, p % 32 >= HD, p == 0, p == 1, p < 2], 1),
        np.tile(np.arange(E), (P, 1)), p[:, None] + T * np.arange(B)[None], N + p[:, None],
        np.tile(np.arange(SLOTS), (P, 1))], axis=1).astype(f)
    cols = np.concatenate([
        chunks(a("L0_xattn_bq")), chunks(a("L0_xattn_bk")), chunks(a("L0_xattn_bv")),
        a("fside_BxS2_0").T, chunks(a("L0_ffn_bs1")),
        a("L0_ffn_b1").reshape(E, HC, P).transpose(2, 0, 1).reshape(P, E * HC),
        a("L0_ffn_gate_w").reshape(DC, P, E).transpose(1, 0, 2).reshape(P, DC * E)], axis=1)
    rows = np.concatenate([
        a("L0_xattn_alpha_pos"), a("L0_xattn_alpha_neg"), a("L0_xattn_gamma").reshape(1),
        a("L0_xattn_delta").reshape(1), a("g_xattn").reshape(1), a("g_ffn").reshape(1),
        a("L0_ffn_gate_b"), a("L0_xattn_bo"), a("L0_ffn_bs2")])[None]
    b2 = a("L0_ffn_b2").reshape(1, E * D)
    w1 = np.concatenate([a("L0_ffn_ws1")[None], a("L0_ffn_w1")]).reshape((1 + E) * D, HID)
    w2 = np.concatenate([a("L0_ffn_ws2")[None], a("L0_ffn_w2")]).reshape((1 + E) * HID, D)

    nc = bacc.Bacc("TRN2", target_bir_lowering=False, num_devices=1)
    arrays, args = {}, []
    for name, v in dict(x=x, ctxT=ctxT, frac=frac, wproj=wproj, consts=consts, cols=cols, rows=rows,
                        b2=b2, w1=w1, w2=w2).items():
        arrays[name] = np.ascontiguousarray(v)
        args.append(nc.dram_tensor(name, v.shape, mybir.dt.from_np(v.dtype), kind="ExternalInput").ap())
    xs_dram = nc.dram_tensor("xs_dram", (SLOTS * P, ROW), mybir.dt.float32).ap()
    out = nc.dram_tensor("out", (N + P, D), mybir.dt.float32, kind="ExternalOutput").ap()
    build(nc, *args, xs_dram, out)
    r = run_bass_kernel_spmd(nc, [arrays], core_ids=[0])
    return r.results[0]["out"][:N].reshape(B, T, D)
```

```python
import concourse.bass as bass
from concourse import mybir
from contextlib import ExitStack

P = 128
B, T, D = 16, 128, 256
H, HD = 16, 16
E, HID = 8, 1024
N = B * T
DC = D // P
HC = HID // P
R = 4
HR = H // R
STEPS = B * R
PAIRS = B // 2
TOPK = 2
TR = 256
TH = TR // P
TILES = N * TOPK // TR + E - 1
GROUPS = N // 512
CLAMP = 0.2
EPS = 1e-5
ROW = D + 2

WS = 2 * 2 * DC * HID
W1H, W1L, W2H, W2L = (k * DC * HID for k in range(4))
EARLY = 6

C_ID, C_UP = 0, P
C_EVEN, C_ODD, C_R0, C_R1, C_R01 = (2 * P + k for k in range(5))
C_IOTA = 2 * P + 5
C_TOK = C_IOTA + E
C_PAD = C_TOK + B
C_TILE = C_PAD + TH
C_N = C_TILE + TILES
K_BQ, K_BK, K_BV, K_FR = 0, DC, 2 * DC, 3 * DC
K_BS1 = K_FR + B
K_B1 = K_BS1 + HC
K_GW = K_B1 + E * HC
K_N = K_GW + DC * E
V_AP, V_AN, V_GAMMA, V_DELTA, V_GX, V_GF = 0, H, 2 * H, 2 * H + 1, 2 * H + 2, 2 * H + 3
V_GB = 2 * H + 4
V_BO = V_GB + E
V_BS2 = V_BO + D
V_N = V_BS2 + D


def head(r, j):
    return 8 * (j // 2) + 2 * r + j % 2


def build(nc, x, ctxT, frac, wproj, consts, cols, rows, b2, w1, w2, xs_dram, out):
    fp32, bf16 = mybir.dt.float32, mybir.dt.bfloat16
    i32, u32 = mybir.dt.int32, mybir.dt.uint32
    ALU, ACT, AX = mybir.AluOpType, mybir.ActivationFunctionType, mybir.AxisListType

    with ExitStack() as ctx:
        def sb(name, shape, dt=fp32):
            return ctx.enter_context(nc.sbuf_tensor(name, shape, dt))

        def sem(name):
            return ctx.enter_context(nc.semaphore(name))

        W = sb("W", [P, (1 + E) * WS], bf16)
        xres = sb("xres", [P, B * D])
        xT2 = sb("xT2", [P, 2 * DC * N], bf16)
        stage = sb("stage", [P, 2 * HID])
        hbuf = sb("hbuf", [P, 2, 512])
        hsplit = sb("hsplit", [P, 2, 2, 512], bf16)
        pay = sb("pay", [P, 2, TOPK, ROW])
        b2hl = sb("b2hl", [P, E * D], bf16)
        cst = sb("cst", [P, C_N])
        col = sb("col", [P, K_N])
        row = sb("row", [P, V_N])
        upb = sb("upb", [P, P], bf16)
        oneb = sb("oneb", [P, P], bf16)
        selb = sb("selb", [P, P], bf16)
        gwhl = sb("gwhl", [P, 2, DC, E], bf16)
        ident = cst[:, C_ID:C_ID + P]

        top = [EARLY * WS]

        def under(n, dt=fp32):
            size = n * (2 if dt == fp32 else 1)
            at = top[0]
            top[0] += size
            assert top[0] <= (1 + E) * WS
            v = W[:, at:at + size]
            return v.bitcast(fp32) if dt == fp32 else v

        sc = [under(HR * T) for _ in range(R)]
        pb = [under(HR * T) for _ in range(R)]
        pth = [under(HR * T, bf16) for _ in range(2)]
        ptl = [under(HR * T, bf16) for _ in range(2)]
        qT = [under(DC * T) for _ in range(2)]
        kz = [under(2 * DC * T) for _ in range(2)]
        vh = [under(D, bf16) for _ in range(2)]
        vl = [under(D, bf16) for _ in range(2)]
        cT = [under(DC * T) for _ in range(2)]
        xh = under(D)
        xhT = under(DC * T)
        on = under(D)
        oT = under(DC * T)
        fr = [under(T) for _ in range(2)]
        dneg = [under(T) for _ in range(2)]
        dd = under(T)
        dpos = under(T)
        wp = under(4 * DC * D)
        bo_t = under(D)

        def wproj_at(k, c):
            return wp[:, (k * DC + c) * D:(k * DC + c + 1) * D]

        xs = [stage[:, k * TH * D:(k + 1) * TH * D] for k in range(2)]
        ysb = [[stage[:, (TH * (2 + k) + t) * D:(TH * (2 + k) + t + 1) * D] for t in range(TH)] for k in range(2)]
        hs = [xT2[:, k * 2 * HC * TR:(k + 1) * 2 * HC * TR] for k in range(2)]
        xsT = [hsplit[:].rearrange("p a b n -> p (a b n)")[:, k * 2 * DC * TR:(k + 1) * 2 * DC * TR] for k in range(2)]

        def pt(name, shape, dt=fp32):
            return sb(name, shape, dt)
        st6 = pt("st6", [P, B, 6])
        mv1 = pt("mv1", [P, B, 2])
        mv2 = pt("mv2", [P, B, 2])
        rstd1 = pt("rstd1", [P, B])
        rstd2 = pt("rstd2", [P, B])
        mhalf = pt("mhalf", [P, B])
        mn = pt("mn", [P, 2, H])
        sm = pt("sm", [P, 2, H])
        rs = pt("rs", [P, H])
        tgx = pt("tgx", [P, 1])
        tgf = pt("tgf", [P, 1])
        gs = pt("gs", [P, 1])
        bqs = pt("bqs", [P, DC])
        bkm = pt("bkm", [P, 2, DC])
        apd = pt("apd", [P, H])
        and_ = pt("and_", [P, H])
        bs2t = row[:, V_BS2:V_BS2 + D]
        parts = hsplit[:].rearrange("p a b n -> p (a b n)")
        lg, mx8, ix8f, oh0, oh1, ca0, ca1, offs = (
            parts[:, k * 256:(k + 1) * 256].bitcast(fp32).rearrange("p (b e) -> p b e", e=E) for k in range(8))
        ix8 = parts[:, 512:768].bitcast(u32).rearrange("p (b e) -> p b e", e=E)
        oh, ca = [oh0, oh1], [ca0, ca1]
        tcmp = hbuf[:].rearrange("p a n -> p (a n)")[:, 0:TILES * E].rearrange("p (j e) -> p j e", e=E)
        ixf = pt("ixf", [P, B, TOPK])
        wt = pt("wt", [P, B, TOPK])
        wid = pt("wid", [P, B, TOPK, 2])
        ed = pt("ed", [P, B])
        meta = pt("meta", [P, TILES * TH, 2])
        posf = pt("posf", [P, TOPK, B])
        posu = pt("posu", [P, TOPK, B], u32)
        place = pt("place", [P, 2, TOPK], u32)
        selm = (hbuf[:].rearrange("p a n -> p (a n)")[:, 512:512 + B * E // 2].bitcast(bf16)
                .rearrange("p (b e) -> p b e", e=E))
        te_i = pt("te_i", [P, E], i32)
        te = [pt(f"te{k}", [P, E]) for k in range(3)]
        tef = pt("tef", [P, TILES])
        tei = pt("tei", [P, TILES], i32)
        b1t = pt("b1t", [P, 2, HC])
        idu = pt("idu", [P, 2, TH], u32)
        padt = pay[:, 0, :, :]

        bank = [ctx.enter_context(nc.psum_tensor(f"bank{k}", [P, 512], fp32)) for k in range(8)]
        psS, psT, psQK, psO, psM, psVY = bank[0:2], bank[2:4], bank[4], bank[5], bank[6], bank[7]

        ld_par, ld_wp, ld_b2 = sem("ld_par"), sem("ld_wp"), sem("ld_b2")
        ld_x = [sem(f"ld_x{k}") for k in range(4)]
        ld_ctx = [sem(f"ld_ctx{k}") for k in range(2)]
        ld_st = [sem(f"ld_st{k}") for k in range(2)]
        pad_ready, pad_written = sem("pad_ready"), sem("pad_written")
        setup_act, setup_dve, setup_pool = sem("setup_act"), sem("setup_dve"), sem("setup_pool")
        ln1_stat, ln1_rstd = sem("ln1_stat"), sem("ln1_rstd")
        b2_done, converted = sem("b2_done"), sem("converted")
        xh_ready, xhT_ps, xhT_ready = sem("xh_ready"), sem("xhT_ps"), sem("xhT_ready")
        qk_ps, qk_ready, v_ps, v_ready = sem("qk_ps"), sem("qk_ready"), sem("v_ps"), sem("v_ready")
        d_ready, pb_ready, xb_ready = sem("d_ready"), sem("pb_ready"), sem("xb_ready")
        s_ps, biased, scored, probs = sem("s_ps"), sem("biased"), sem("scored"), sem("probs")
        pt_ps, pt_hi, pt_lo, pv = sem("pt_ps"), sem("pt_hi"), sem("pt_lo"), sem("pv")
        o_ready, oT_ps, oT_ready, y_ps, x1_ready = (sem("o_ready"), sem("oT_ps"), sem("oT_ready"),
                                                    sem("y_ps"), sem("x1_ready"))
        dve_own, pool_own, act_own = sem("dve_own"), sem("pool_own"), sem("act_own")
        ln2_stat, ln2_rstd = sem("ln2_stat"), sem("ln2_rstd")
        xh2_ready, x2T_ps, x2_hi, x2_lo, gate_ps, gated = (sem("xh2_ready"), sem("x2T_ps"), sem("x2_hi"),
                                                         sem("x2_lo"), sem("gate_ps"), sem("gated"))
        wd_ready, we_ready, sel_ready, rank_ps, routed = (sem("wd_ready"), sem("we_ready"), sem("sel_ready"),
                                                        sem("rank_ps"), sem("routed"))
        pay_ready = sem("pay_ready")
        dispatched = [sem(f"dispatched{k}") for k in range(2)]
        su_ps, sg_ready, sh_ready, sd_used, sy_ps, acc_ready = (sem("su_ps"), sem("sg_ready"), sem("sh_ready"),
                                                              sem("sd_used"), sem("sy_ps"), sem("acc_ready"))
        out_written = sem("out_written")
        xs_in = [sem(f"xs_in{k}") for k in range(2)]
        xsT_ps, xs_hi, xs_lo, meta_in = sem("xsT_ps"), sem("xs_hi"), sem("xs_lo"), sem("meta_in")
        b1_ready, up_ps, g_ready, h_ready, down_ps, y_ready = (sem("b1_ready"), sem("up_ps"), sem("g_ready"),
                                                               sem("h_ready"), sem("down_ps"), sem("y_ready"))
        added = [sem(f"added{k}") for k in range(2)]
        dpos_done, dneg_done, conv_hi = sem("dpos_done"), sem("dneg_done"), sem("conv_hi")
        vh_done, rs_done, st_done, sh_hi, h_hi, acc_half = (sem("vh_done"), sem("rs_done"), sem("st_done"),
                                                          sem("sh_hi"), sem("h_hi"), sem("acc_half"))

        def pairs(eng, body):
            body(0, 0)
            body(1, 1)
            with eng.Fori(1, PAIRS - 1) as i:
                body(2 * i, 0)
                body(2 * i + 1, 1)
            body(B - 2, 0)
            body(B - 1, 1)

        passed = {}

        def wait_alone(eng, name, s, value):
            if name not in passed:
                passed[name] = sem(f"passed_{name}")
            eng.wait_ge(s, value)
            eng.sem_inc(passed[name], 1)

        def tiles(eng, body):
            body(0, 0, 2)
            body(1, 1, 2)
            with eng.Fori(1, TILES // 2 - 1) as i:
                body(2 * i, 0, 2)
                body(2 * i + 1, 1, 2)
            for j in range(TILES - 3, TILES):
                body(j, j % 2, min(2, TILES - 1 - j))

        def first(b, n=1):
            return isinstance(b, int) and b < n

        def last(b):
            return isinstance(b, int) and b == B - 1

        block = ctx.enter_context(nc.Block())

        @block.sync
        def _(sp):
            sp.dma_start(cst[:], consts).then_inc(ld_par, 16)
            sp.dma_start(col[:], cols).then_inc(ld_par, 16)
            sp.dma_start(row[:], rows.to_broadcast([P, V_N])).then_inc(ld_par, 16)
            for k in range(4):
                sp.dma_start(xres[:, k * 4 * D:(k + 1) * 4 * D].rearrange("p (b d) -> p b d", d=D),
                             x[4 * k:4 * k + 4].rearrange("b p d -> p b d")).then_inc(ld_x[k], 16)
            sp.dma_start(wp.rearrange("p (k d) -> p k d", d=D), wproj.rearrange("k (c p) d -> p (k c) d", p=P)).then_inc(ld_wp, 16)

            def load_seq(b, par):
                if not first(b, 2):
                    sp.wait_ge(v_ps, b - 1)
                    sp.wait_ge(d_ready, b - 1)
                sp.dma_start(cT[par].rearrange("p (c t) -> p c t", c=DC),
                             ctxT[:, :, bass.ds(b * T, T)].rearrange("c p t -> p c t")).then_inc(ld_ctx[par], 16)
                sp.dma_start(fr[par], frac[:, bass.ds(b * T, T)].to_broadcast([P, T])).then_inc(ld_ctx[par], 16)

            load_seq(0, 0)
            load_seq(1, 1)
            sp.dma_start(stage[:], b2.to_broadcast([P, E * D])).then_inc(ld_b2, 16)
            sp.wait_ge(pad_ready, 1)
            for k in range(TH):
                sp.dma_start(xs_dram.rearrange("(j k p) d -> k p j d", k=TH, p=P)[k],
                             padt[:, k:k + 1, :].to_broadcast([P, TILES, ROW])).then_inc(pad_written, 16)
                sp.dma_start(out[N + k * P:N + (k + 1) * P, :], padt[:, 0, 0:D]).then_inc(pad_written, 16)

            def load_weights(s, half):
                for k in range(2):
                    if not (isinstance(s, int) and s == 0 and half == 0):
                        sp.wait_ge(converted, 4 * s + 2 * half + k - 1)
                    if half == 0:
                        sp.dma_start(stage[:, k * HID:(k + 1) * HID],
                                     w1[bass.ds(s * D + k * P, P), :]).then_inc(ld_st[k], 16)
                    else:
                        sp.dma_start(stage[:, k * HID:(k + 1) * HID].rearrange("p (c d) -> p c d", d=D),
                                     w2[bass.ds(s * HID + k * 4 * P, 4 * P), :]
                                     .rearrange("(c p) d -> p c d", p=P)).then_inc(ld_st[k], 16)

            sp.wait_ge(b2_done, 1)
            load_weights(0, 0)
            load_weights(0, 1)
            with sp.Fori(1, EARLY) as i:
                load_seq(2 * i, 0)
                load_seq(2 * i + 1, 1)
                load_weights(i, 0)
                load_weights(i, 1)
            with sp.Fori(EARLY, PAIRS) as i:
                load_seq(2 * i, 0)
                load_seq(2 * i + 1, 1)
            with sp.Fori(EARLY, 1 + E) as s:
                load_weights(s, 0)
                load_weights(s, 1)

            with sp.Fori(0, GROUPS) as g:
                sp.wait_ge(acc_ready, 4 * g + 4)
                sp.dma_start(out[bass.ds(g * 512, 512), :].rearrange("(t p) d -> p t d", p=P),
                             xres[:, bass.ds(g * 4 * D, 4 * D)].rearrange("p (t d) -> p t d", d=D)).then_inc(out_written, 16)

            for k in range(2):
                sp.wait_ge(dispatched[k], 16 * TOPK * B // 2)
            sp.wait_ge(converted, 4 * (1 + E))

            def load_tile(j, par):
                if not first(j, 2):
                    sp.wait_ge(xsT_ps, j - 1)
                sp.dma_start(xs[par].rearrange("p (t d) -> p t d", d=D),
                             xs_dram[bass.ds(j * TR, TR), 0:D].rearrange("(t p) d -> p t d", p=P)).then_inc(xs_in[par], 16)

            load_tile(0, 0)
            load_tile(1, 1)
            sp.dma_start(meta[:], xs_dram.rearrange("(j p) d -> p j d", p=P)[:, :, D:ROW]).then_inc(meta_in, 16)
            with sp.Fori(1, TILES // 2) as i:
                load_tile(2 * i, 0)
                load_tile(2 * i + 1, 1)
            load_tile(TILES - 1, 0)

        @block.gpsimd
        def _(pool):
            own = [0]

            def link(ins):
                own[0] += 1
                ins.then_inc(pool_own, 1)
                pool.wait_ge(pool_own, own[0])

            link(nc.gpsimd.memset(mhalf[:], -0.5))
            nc.gpsimd.memset(padt, 0.0).then_inc(pool_own, 1)
            own[0] += 1
            pool.wait_ge(pool_own, own[0])
            pool.wait_ge(ld_par, 48)
            nc.gpsimd.tensor_copy(padt[:, :, D + 1:D + 2], cst[:, C_PAD:C_PAD + TH].rearrange("p (k o) -> p k o", o=1)).then_inc(pad_ready, 1)
            pool.wait_ge(setup_act, 2)
            link(nc.gpsimd.tensor_scalar(bo_t, row[:, V_BO:V_BO + D], tgx[:, 0:1], None, ALU.mult))
            nc.gpsimd.tensor_scalar(bs2t, row[:, V_BS2:V_BS2 + D], tgf[:, 0:1], None, ALU.mult).then_inc(setup_pool, 1)
            pool.wait_ge(ln1_stat, B)
            link(nc.gpsimd.tensor_scalar(rstd1[:], mv1[:, :, 1], EPS, None, ALU.add))
            nc.gpsimd.tensor_tensor(rstd1[:], rstd1[:], mhalf[:], ALU.pow).then_inc(ln1_rstd, 1)
            pool.wait_ge(setup_dve, 1)

            def seq(b, par):
                i = b // 2 if isinstance(b, int) else None
                if isinstance(b, int):
                    pool.wait_ge(ld_ctx[par], 32 * (i + 1))
                else:
                    pool.wait_ge(ld_ctx[par], 16 * (b - par) + 32)
                if not first(b):
                    pool.wait_ge(pb_ready, R * b)
                nc.gpsimd.tensor_tensor(dd, fr[par], col[:, bass.ds(K_FR + b, 1)].to_broadcast([P, T]), ALU.subtract).then_inc(d_ready, 1)
                wait_alone(pool, "pool", d_ready, b + 1)
                nc.gpsimd.tensor_scalar(dpos, dd, 0.0, CLAMP, ALU.max, ALU.min).then_inc(dpos_done, 1)
                if not first(b, 2):
                    wait_alone(pool, "pool", biased, R * (b - 1))
                nc.gpsimd.tensor_scalar(dneg[par], dd, 0.0, -CLAMP, ALU.min, ALU.max).then_inc(dneg_done, 1)
                wait_alone(pool, "pool", dpos_done, b + 1)
                for r in range(R):
                    if not first(b):
                        wait_alone(pool, "pool", scored, R * b + r - 3)
                    for j in range(HR):
                        h = head(r, j)
                        ins = nc.gpsimd.tensor_scalar(pb[r][:, j * T:(j + 1) * T], dpos, apd[:, h:h + 1], None, ALU.mult)
                    ins.then_inc(pb_ready, 1)
                pool.wait_ge(xh_ready, b + 1)
                xb = xres[:, bass.ds(b * D, D)]
                nc.gpsimd.tensor_tensor(xb, xb, bo_t, ALU.add).then_inc(xb_ready, 1)

            def convert(s, half):
                for k in range(2):
                    base = s * WS + (W2H if half else W1H) + k * HID
                    hi = W[:, bass.ds(base, HID)]
                    lo = W[:, bass.ds(base + DC * HID, HID)]
                    src = stage[:, k * HID:(k + 1) * HID]
                    pool.wait_ge(ld_st[k], 32 * s + 16 * half + 16)
                    nc.gpsimd.tensor_copy(hi, src).then_inc(conv_hi, 1)
                    pool.wait_ge(conv_hi, 4 * s + 2 * half + k + 1)
                    nc.gpsimd.tensor_tensor(lo, src, hi, ALU.subtract).then_inc(converted, 1)

            def both(b, par, s=None):
                seq(b, par)
                if s is not None:
                    convert(s, par)

            for par in range(2):
                both(par, par, 0)
            with pool.Fori(1, EARLY) as i:
                for par in range(2):
                    both(2 * i + par, par, i)
            with pool.Fori(EARLY, PAIRS) as i:
                for par in range(2):
                    both(2 * i + par, par)

            pool.wait_ge(ln2_stat, B)
            own[0] += 1
            nc.gpsimd.tensor_scalar(rstd2[:], mv2[:, :, 1], EPS, None, ALU.add).then_inc(pool_own, 1)
            pool.wait_ge(pool_own, own[0])
            nc.gpsimd.tensor_tensor(rstd2[:], rstd2[:], mhalf[:], ALU.pow).then_inc(ln2_rstd, 1)

            pool.wait_ge(x1_ready, B)
            with pool.Fori(EARLY, 1 + E) as s:
                convert(s, 0)
                convert(s, 1)

            pool.wait_ge(pad_written, 32 * TH)
            with pool.Fori(0, PAIRS) as i:
                for par in range(2):
                    b = 2 * i + par
                    wait_alone(pool, "pool", pay_ready, b + 1)
                    for k in range(TOPK):
                        nc.gpsimd.indirect_dma_start(
                            xs_dram, bass.IndirectOffsetOnAxis(place[:, par, k:k + 1], axis=0),
                            pay[:, par, k, :], None).then_inc(dispatched[par], 16)

            pool.wait_ge(out_written, 16 * GROUPS)

            def add_tile(j, par):
                wait_alone(pool, "pool", y_ready, j + 1)
                for t in range(TH):
                    if t > 0:
                        wait_alone(pool, "pool", added[t - 1], 16 * (j + 1))
                    elif not first(j):
                        wait_alone(pool, "pool", added[TH - 1], 16 * j)
                    nc.gpsimd.indirect_dma_start(
                        out, bass.IndirectOffsetOnAxis(idu[:, par, t:t + 1], axis=0),
                        ysb[par][t], None, compute_op=ALU.add).then_inc(added[t], 16)

            add_tile(0, 0)
            add_tile(1, 1)
            with pool.Fori(1, TILES // 2) as i:
                add_tile(2 * i, 0)
                add_tile(2 * i + 1, 1)
            add_tile(TILES - 1, 0)
            for t in range(TH):
                pool.wait_ge(added[t], 16 * TILES)

        @block.scalar
        def _(act):
            act.wait_ge(ld_par, 48)
            nc.scalar.activation(tgx[:], row[:, V_GX:V_GX + 1], ACT.Tanh).then_inc(setup_act, 1)
            nc.scalar.activation(tgf[:], row[:, V_GF:V_GF + 1], ACT.Tanh).then_inc(setup_act, 1)
            act.wait_ge(setup_dve, 1)

            def move_xhT(b):
                act.wait_ge(xhT_ps, b + 1)
                if not first(b):
                    act.wait_ge(v_ps, b)
                nc.scalar.activation(xhT, psM[:, 0:DC * T], ACT.Copy).then_inc(xhT_ready, 1)

            def move_q(b, par):
                act.wait_ge(qk_ps, b + 1)
                if not first(b, 2):
                    act.wait_ge(s_ps, R * (b - 1))
                for c in range(DC):
                    nc.scalar.activation(qT[par][:, c * T:(c + 1) * T], psQK[:, c * T:(c + 1) * T], ACT.Identity,
                                         scale=gs[:, 0:1], bias=bqs[:, c:c + 1])

            def move_k(b, par):
                for e in range(2):
                    for c in range(DC):
                        ins = nc.scalar.activation(
                            kz[par][:, (e * DC + c) * T:(e * DC + c + 1) * T],
                            psQK[:, (DC + c) * T:(DC + c + 1) * T], ACT.Identity,
                            scale=cst[:, C_EVEN + e:C_EVEN + e + 1], bias=bkm[:, e, c:c + 1])
                ins.then_inc(qk_ready, 1)

            def high(n, k, wait_free):
                act.wait_ge(pt_ps, n + 1)
                if wait_free:
                    act.wait_ge(pv, n - 1)
                nc.scalar.activation(pth[k], psT[k][:], ACT.Copy).then_inc(pt_hi, 1)

            def exps(n, r, par):
                act.wait_ge(scored, n + 1)
                for j in range(HR):
                    q = r * HR + j
                    ins = nc.scalar.activation(sc[r][:, j * T:(j + 1) * T], sc[r][:, j * T:(j + 1) * T], ACT.Exp,
                                               scale=-1.0, bias=mn[:, par, q:q + 1], accum_out=sm[:, par, q:q + 1])
                ins.then_inc(probs, 1)

            def move_oT(b):
                act.wait_ge(oT_ps, b + 1)
                if not first(b):
                    act.wait_ge(y_ps, b)
                for c in range(DC):
                    ins = nc.scalar.activation(oT[:, c * T:(c + 1) * T], psM[:, c * T:(c + 1) * T], ACT.Identity,
                                               bias=col[:, K_BV + c:K_BV + c + 1])
                ins.then_inc(oT_ready, 1)

            def seq(b, par):
                for r in range(R):
                    n = R * b + r
                    if not (first(b) and r == 0):
                        high(n - 1, (r - 1) % 2, not (first(b) and r < 3))
                    if r == 3 and not first(b):
                        move_oT(b - 1)
                    if r == 0 and not first(b, 2):
                        act.wait_ge(o_ready, b - 1)
                    exps(n, r, par)
                    if not last(b):
                        if r == 0:
                            move_xhT(b + 1)
                        if r == 1:
                            move_q(b + 1, 1 - par)
                        if r == 2:
                            move_k(b + 1, 1 - par)

            move_xhT(0)
            move_q(0, 0)
            move_k(0, 0)
            pairs(act, seq)
            high(STEPS - 1, 1, True)
            move_oT(B - 1)

            def high2(b, par):
                act.wait_ge(x2T_ps, b + 1)
                nc.scalar.activation(xT2[:, 0:DC * N].rearrange("p (c n) -> p c n", c=DC)[:, :, bass.ds(b * T, T)],
                                     bank[6 + par][:, 0:DC * T].rearrange("p (c t) -> p c t", c=DC), ACT.Copy).then_inc(x2_hi, 1)

            with act.Fori(0, PAIRS) as i:
                high2(2 * i, 0)
                high2(2 * i + 1, 1)
            act.wait_ge(wd_ready, 1)
            nc.scalar.activation(ed[:], ed[:], ACT.Exp).then_inc(we_ready, 1)

            def gelu_shared(g):
                for c in range(HC):
                    act.wait_ge(su_ps, HC * g + c + 1)
                    if not (first(g) and c < 2):
                        act.wait_ge(sh_ready, HC * g + c - 1)
                    nc.scalar.activation(hbuf[:, c % 2, :], bank[c % 2][:], ACT.Gelu,
                                         bias=col[:, K_BS1 + c:K_BS1 + c + 1]).then_inc(sg_ready, 1)

            gelu_shared(0)
            with act.Fori(1, GROUPS) as g:
                gelu_shared(g)

            def high_tile(j, par):
                act.wait_ge(xsT_ps, j + 1)
                if not first(j, 2):
                    act.wait_ge(up_ps, 4 * (j - 1))
                nc.scalar.activation(xsT[par][:, 0:DC * TR], bank[6 + par][:, 0:DC * TR], ACT.Copy).then_inc(xs_hi, 1)

            def gelu_tile(j, par):
                act.wait_ge(b1_ready, j + 1)
                for q in range(4):
                    act.wait_ge(up_ps, 4 * j + q + 1)
                    if not (first(j) and q < 2):
                        act.wait_ge(h_ready, 4 * j + q - 1)
                    for c in range(2):
                        ins = nc.scalar.activation(hbuf[:, q % 2, c * TR:(c + 1) * TR], bank[q][:, c * TR:(c + 1) * TR],
                                                   ACT.Gelu, bias=b1t[:, par, 2 * q + c:2 * q + c + 1])
                    ins.then_inc(g_ready, 1)

            def body(j, par, more):
                gelu_tile(j, par)
                if more == 2:
                    high_tile(j + 2, par)

            act.wait_ge(sy_ps, GROUPS)
            high_tile(0, 0)
            high_tile(1, 1)
            tiles(act, body)

        @block.vector
        def _(dve):
            own = [0]

            def link(ins):
                own[0] += 1
                ins.then_inc(dve_own, 1)
                dve.wait_ge(dve_own, own[0])

            dve.wait_ge(ld_par, 48)
            link(nc.vector.tensor_scalar(gs[:], row[:, V_GAMMA:V_GAMMA + 1], -(HD ** -0.5), None, ALU.mult))
            link(nc.vector.tensor_scalar(bqs[:], col[:, K_BQ:K_BQ + DC], gs[:, 0:1], None, ALU.mult))
            for e in range(2):
                link(nc.vector.tensor_scalar(bkm[:, e, :], col[:, K_BK:K_BK + DC], cst[:, C_EVEN + e:C_EVEN + e + 1], None, ALU.mult))
            link(nc.vector.tensor_scalar(apd[:], row[:, V_AP:V_AP + H], row[:, V_DELTA:V_DELTA + 1], -1.0, ALU.mult, ALU.mult))
            link(nc.vector.tensor_scalar(and_[:], row[:, V_AN:V_AN + H], row[:, V_DELTA:V_DELTA + 1], -1.0, ALU.mult, ALU.mult))
            gw = col[:, K_GW:K_GW + DC * E].rearrange("p (c e) -> p c e", c=DC)
            link(nc.vector.tensor_copy(gwhl[:, 0], gw))
            link(nc.vector.tensor_tensor(gwhl[:, 1], gw, gwhl[:, 0], ALU.subtract))
            link(nc.vector.tensor_copy(upb[:], cst[:, C_UP:C_UP + P]))
            link(nc.vector.memset(oneb[:], 1.0))
            nc.vector.tensor_copy(selb[:], cst[:, C_R01:C_R01 + 1].to_broadcast([P, P])).then_inc(setup_dve, 1)
            for b in range(B):
                if b % 4 == 0:
                    dve.wait_ge(ld_x[b // 4], 16)
                link(nc.vector.bn_stats(st6[:, b, :], xres[:, b * D:(b + 1) * D]))
                nc.vector.bn_aggr(mv1[:, b, :], st6[:, b, :]).then_inc(ln1_stat, 1)

            def norm1(b):
                if first(b):
                    dve.wait_ge(ln1_rstd, 1)
                else:
                    dve.wait_ge(xhT_ps, b)
                nc.vector.tensor_scalar(xh, xres[:, bass.ds(b * D, D)], mv1[:, bass.ds(b, 1), 0], rstd1[:, bass.ds(b, 1)],
                                        ALU.subtract, ALU.mult).then_inc(xh_ready, 1)

            def values(b, par):
                dve.wait_ge(v_ps, b + 1)
                if not first(b, 2):
                    dve.wait_ge(pv, R * (b - 1))
                nc.vector.tensor_copy(vh[par], psVY[:, 0:D]).then_inc(vh_done, 1)
                dve.wait_ge(vh_done, b + 1)
                nc.vector.tensor_tensor(vl[par], psVY[:, 0:D], vh[par], ALU.subtract).then_inc(v_ready, 1)

            def bias(n, r, par, b):
                dve.wait_ge(s_ps, n + 1)
                if r == 0:
                    dve.wait_ge(dneg_done, b + 1)
                if not first(b):
                    dve.wait_ge(pt_ps, n - 3)
                for j in range(HR):
                    h = head(r, j)
                    ins = nc.vector.scalar_tensor_tensor(sc[r][:, j * T:(j + 1) * T], dneg[par], and_[:, h:h + 1],
                                                         psS[r % 2][:, j * T:(j + 1) * T], ALU.mult, ALU.add)
                ins.then_inc(biased, 1)

            def low(n, k, wait_free):
                dve.wait_ge(pt_hi, n + 1)
                if wait_free:
                    dve.wait_ge(pv, n - 1)
                nc.vector.tensor_tensor(ptl[k], psT[k][:], pth[k], ALU.subtract).then_inc(pt_lo, 1)

            def least(n, r, par, b):
                dve.wait_ge(pb_ready, n + 1)
                if not first(b, 2):
                    dve.wait_ge(probs, n - 7)
                wait_alone(dve, "dve", biased, n + 1)
                for j in range(HR):
                    s = sc[r][:, j * T:(j + 1) * T]
                    q = r * HR + j
                    ins = nc.vector.tensor_tensor_reduce(out=s, in0=s, in1=pb[r][:, j * T:(j + 1) * T], scale=1.0,
                                                         scalar=3.0e38, op0=ALU.add, op1=ALU.min, accum_out=mn[:, par, q:q + 1])
                ins.then_inc(scored, 1)

            def output(b, par):
                dve.wait_ge(pv, R * b + R)
                if not first(b):
                    dve.wait_ge(oT_ps, b)
                nc.vector.reciprocal(rs[:], sm[:, par, :]).then_inc(rs_done, 1)
                dve.wait_ge(rs_done, b + 1)
                for c in range(DC):
                    ins = nc.vector.tensor_tensor(
                        on[:, c * P:(c + 1) * P].rearrange("p (r e d) -> p r e d", r=R, e=2),
                        psO[:, c * P:(c + 1) * P].rearrange("p (r e d) -> p r e d", r=R, e=2),
                        rs[:].rearrange("p (r c e o) -> p c r e o", r=R, c=DC, o=1)[:, c].to_broadcast([P, R, 2, HD]),
                        ALU.mult)
                ins.then_inc(o_ready, 1)

            def residual(b):
                dve.wait_ge(y_ps, b + 1)
                dve.wait_ge(xb_ready, b + 1)
                xb = xres[:, bass.ds(b * D, D)]
                nc.vector.scalar_tensor_tensor(xb, psVY[:, D:2 * D], tgx[:, 0:1], xb, ALU.mult, ALU.add).then_inc(x1_ready, 1)
                wait_alone(dve, "dve", x1_ready, b + 1)
                nc.vector.bn_stats(st6[:, bass.ds(b, 1), :].rearrange("p b k -> p (b k)"), xb).then_inc(st_done, 1)

            def seq(b, par):
                if not last(b):
                    norm1(b + 1)
                for r in range(R):
                    n = R * b + r
                    bias(n, r, par, b)
                    if r == 1 and not first(b):
                        output(b - 1, 1 - par)
                    if r == 2 and not last(b):
                        values(b + 1, 1 - par)
                    if not (first(b) and r == 0):
                        low(n - 1, (r - 1) % 2, not (first(b) and r < 3))
                    least(n, r, par, b)
                    if r == 3 and not first(b):
                        residual(b - 1)

            norm1(0)
            values(0, 0)
            dve.wait_ge(ld_b2, 16)
            link(nc.vector.tensor_copy(b2hl[:], stage[:]))
            link(nc.vector.tensor_tensor(stage[:], stage[:], b2hl[:], ALU.subtract))
            link(nc.vector.tensor_scalar(b2hl[:], b2hl[:], cst[:, C_R0:C_R0 + 1], None, ALU.mult))
            nc.vector.scalar_tensor_tensor(b2hl[:], stage[:], cst[:, C_R1:C_R1 + 1], b2hl[:], ALU.mult, ALU.add).then_inc(b2_done, 1)
            pairs(dve, seq)
            low(STEPS - 1, 1, True)
            output(B - 1, 1)
            residual(B - 1)
            dve.wait_ge(st_done, B)
            for b in range(B):
                nc.vector.bn_aggr(mv2[:, b, :], st6[:, b, :]).then_inc(ln2_stat, 1)

            dve.wait_ge(ln2_rstd, 1)

            def norm2(b, par):
                dve.wait_ge(x2T_ps, b - 1) if not first(b, 2) else None
                nc.vector.tensor_scalar(hbuf[:, par, 0:D], xres[:, bass.ds(b * D, D)], mv2[:, bass.ds(b, 1), 0],
                                        rstd2[:, bass.ds(b, 1)], ALU.subtract, ALU.mult).then_inc(xh2_ready, 1)

            def low2(b, par):
                dve.wait_ge(x2_hi, b + 1)
                xT = xT2[:, :].rearrange("p (k c n) -> p k c n", k=2, c=DC)
                nc.vector.tensor_tensor(xT[:, 1, :, bass.ds(b * T, T)],
                                        bank[6 + par][:, 0:DC * T].rearrange("p (c t) -> p c t", c=DC),
                                        xT[:, 0, :, bass.ds(b * T, T)], ALU.subtract).then_inc(x2_lo, 1)

            norm2(0, 0)
            norm2(1, 1)
            with dve.Fori(1, PAIRS) as i:
                for par in range(2):
                    low2(2 * i + par - 2, par)
                    norm2(2 * i + par, par)
            low2(B - 2, 0)
            low2(B - 1, 1)

            dve.wait_ge(gate_ps, 1)
            link(nc.vector.tensor_tensor(lg, bank[4][:, 0:B * E].rearrange("p (b e) -> p b e", e=E),
                                         row[:, V_GB:V_GB + E].rearrange("p (o e) -> p o e", o=1).to_broadcast([P, B, E]), ALU.add))
            for b in range(B):
                ins = nc.vector.max(mx8[:, b, :], lg[:, b, :])
            link(ins)
            for b in range(B):
                ins = nc.vector.max_index(ix8[:, b, :], mx8[:, b, :], lg[:, b, :])
            link(ins)
            nc.vector.tensor_tensor(ed[:], mx8[:, :, 1], mx8[:, :, 0], ALU.subtract).then_inc(wd_ready, 1)
            link(nc.vector.tensor_copy(ixf[:], ix8[:, :, 0:TOPK]))
            iota = cst[:, C_IOTA:C_IOTA + E].rearrange("p (o e) -> p o e", o=1).to_broadcast([P, B, E])
            for k in range(TOPK):
                link(nc.vector.tensor_tensor(oh[k], iota, ixf[:, :, k:k + 1].to_broadcast([P, B, E]), ALU.is_equal))
            nc.vector.tensor_tensor(selm, oh[0], oh[1], ALU.add).then_inc(sel_ready, 1)
            dve.wait_ge(we_ready, 1)
            link(nc.vector.tensor_scalar(wt[:, :, 1], ed[:], 1.0, None, ALU.add))
            link(nc.vector.reciprocal(wt[:, :, 0], wt[:, :, 1]))
            link(nc.vector.tensor_tensor(wt[:, :, 1], ed[:], wt[:, :, 0], ALU.mult))
            link(nc.vector.tensor_scalar(wid[:, :, :, 0], wt[:], tgf[:, 0:1], None, ALU.mult))
            for k in range(TOPK):
                link(nc.vector.tensor_copy(wid[:, :, k, 1], cst[:, C_TOK:C_TOK + B]))
            dve.wait_ge(rank_ps, 1)
            cnt = bank[5][:, B * E:2 * B * E].rearrange("p (b e) -> p b e", e=E)
            link(nc.vector.tensor_copy(ca[0], cnt))
            a = 0
            step = 1
            while step < B:
                link(nc.vector.tensor_copy(ca[1 - a][:, 0:step, :], ca[a][:, 0:step, :]))
                link(nc.vector.tensor_tensor(ca[1 - a][:, step:B, :], ca[a][:, step:B, :], ca[a][:, 0:B - step, :], ALU.add))
                a, step = 1 - a, 2 * step
            link(nc.vector.tensor_tensor(offs, ca[a], cnt, ALU.subtract))
            link(nc.vector.tensor_scalar(te_i[:], ca[a][:, B - 1, :], float(TR - 1), None, ALU.add))
            link(nc.vector.tensor_single_scalar(te_i[:], te_i[:], TR.bit_length() - 1, op=ALU.arith_shift_right))
            link(nc.vector.tensor_copy(te[0][:], te_i[:]))
            link(nc.vector.tensor_copy(te[1][:], te[0][:]))
            k, step = 1, 1
            while step < E:
                link(nc.vector.tensor_copy(te[3 - k][:, 0:step], te[k][:, 0:step]))
                link(nc.vector.tensor_tensor(te[3 - k][:, step:E], te[k][:, step:E], te[k][:, 0:E - step], ALU.add))
                k, step = 3 - k, 2 * step
            ends, base = te[k], te[3 - k]
            link(nc.vector.tensor_tensor(
                tcmp, cst[:, C_TILE:C_TILE + TILES].rearrange("p (j o) -> p j o", o=1).to_broadcast([P, TILES, E]),
                ends[:].rearrange("p (o e) -> p o e", o=1).to_broadcast([P, TILES, E]), ALU.is_ge))
            link(nc.vector.tensor_reduce(tef[:], tcmp, AX.X, ALU.add))
            link(nc.vector.tensor_scalar(tei[:], tef[:], float(E - 1), None, ALU.min))
            link(nc.vector.tensor_tensor(base[:], ends[:], te[0][:], ALU.subtract))
            link(nc.vector.tensor_scalar(base[:], base[:], float(TR), None, ALU.mult))
            link(nc.vector.tensor_tensor(offs, offs, bank[5][:, 0:B * E].rearrange("p (b e) -> p b e", e=E), ALU.add))
            link(nc.vector.tensor_tensor(offs, offs, base[:].rearrange("p (o e) -> p o e", o=1).to_broadcast([P, B, E]), ALU.add))
            for k in range(TOPK):
                link(nc.vector.tensor_tensor(ca[0], offs, oh[k], ALU.mult))
                link(nc.vector.tensor_reduce(posf[:, k, :], ca[0], AX.X, ALU.add))
            nc.vector.tensor_copy(posu[:], posf[:]).then_inc(routed, 1)
            dve.wait_ge(routed, 1)
            dve.wait_ge(pad_written, 32 * TH)

            def payload(b, par, k, m):
                if k == 0:
                    nc.vector.tensor_copy(place[:, par, :], posu[:, :, bass.ds(b, 1)].rearrange("p k b -> p (k b)"))
                nc.vector.tensor_scalar(pay[:, par, k, 0:D], xres[:, bass.ds(b * D, D)], mv2[:, bass.ds(b, 1), 0],
                                        rstd2[:, bass.ds(b, 1)], ALU.subtract, ALU.mult)
                ins = nc.vector.tensor_copy(pay[:, par, k, D:ROW], wid[:, bass.ds(b, 1), k, :].rearrange("p b k -> p (b k)"))
                if k == 1:
                    ins.then_inc(pay_ready, 1)

            def shared_group(g, y):
                for c in range(HC):
                    m = HC * g + c
                    dve.wait_ge(sg_ready, m + 1)
                    if not (first(g) and c < 2):
                        dve.wait_ge(sd_used, m - 1)
                    nc.vector.tensor_copy(hsplit[:, c % 2, 0, :], hbuf[:, c % 2, :]).then_inc(sh_hi, 1)
                    dve.wait_ge(sh_hi, m + 1)
                    nc.vector.tensor_tensor(hsplit[:, c % 2, 1, :], hbuf[:, c % 2, :], hsplit[:, c % 2, 0, :],
                                            ALU.subtract).then_inc(sh_ready, 1)
                    b, k = 4 * g + c // 2, c % 2
                    par = (c // 2) % 2
                    if k == 0 and not (first(g) and c < 4):
                        dve.wait_ge(dispatched[par], 16 * (4 * g + c // 2 - par))
                    payload(b, par, k, m)
                dve.wait_ge(sy_ps, g + 1)
                for t in range(4):
                    xb = xres[:, bass.ds((4 * g + t) * D, D)]
                    nc.vector.scalar_tensor_tensor(xb, bank[2 + 2 * y + t // 2][:, (t % 2) * D:(t % 2 + 1) * D], tgf[:, 0:1], xb,
                                                   ALU.mult, ALU.add).then_inc(acc_half, 1)
                dve.wait_ge(acc_half, 4 * g + 4)
                dve.wait_ge(setup_pool, 1)
                for t in range(4):
                    xb = xres[:, bass.ds((4 * g + t) * D, D)]
                    nc.vector.tensor_tensor(xb, xb, bs2t, ALU.add).then_inc(acc_ready, 1)

            shared_group(0, 0)
            shared_group(1, 1)
            with dve.Fori(1, GROUPS // 2) as i:
                shared_group(2 * i, 0)
                shared_group(2 * i + 1, 1)

            def bias_tile(j, par):
                e = dve.value_load(tei[0:1, bass.ds(j, 1)], min_val=0, max_val=E - 1)
                if not first(j, 2):
                    dve.wait_ge(g_ready, 4 * (j - 1))
                nc.vector.tensor_copy(b1t[:, par, :], col[:, bass.ds(K_B1 + e * HC, HC)]).then_inc(b1_ready, 1)

            def low_tile(j, par):
                dve.wait_ge(xs_hi, j + 1)
                if not first(j, 2):
                    dve.wait_ge(up_ps, 4 * (j - 1))
                nc.vector.tensor_tensor(xsT[par][:, DC * TR:2 * DC * TR], bank[6 + par][:, 0:DC * TR], xsT[par][:, 0:DC * TR],
                                        ALU.subtract).then_inc(xs_lo, 1)

            def split_tile(j, par):
                for q in range(4):
                    dve.wait_ge(g_ready, 4 * j + q + 1)
                    if q == 0 and not first(j, 2):
                        dve.wait_ge(down_ps, j - 1)
                    hi = hs[par][:, 2 * q * TR:2 * (q + 1) * TR]
                    lo = hs[par][:, (HC + 2 * q) * TR:(HC + 2 * q + 2) * TR]
                    nc.vector.tensor_copy(hi, hbuf[:, q % 2, :]).then_inc(h_hi, 1)
                    dve.wait_ge(h_hi, 4 * j + q + 1)
                    nc.vector.tensor_tensor(lo, hbuf[:, q % 2, :], hi, ALU.subtract).then_inc(h_ready, 1)

            def weigh(j, par):
                dve.wait_ge(down_ps, j + 1)
                if not first(j, 2):
                    dve.wait_ge(added[TH - 1], 16 * (j - 1))
                m = meta[:, bass.ds(j * TH, TH), :]
                nc.vector.tensor_copy(idu[:, par, :], m[:, :, 1])
                for t in range(TH):
                    ins = nc.vector.tensor_scalar(ysb[par][t], bank[4 + par][:, t * D:(t + 1) * D], m[:, t, 0:1], None, ALU.mult)
                ins.then_inc(y_ready, 1)

            def body(j, par, more):
                if more:
                    bias_tile(j + 1, 1 - par)
                split_tile(j, par)
                if more == 2:
                    low_tile(j + 2, par)
                if not first(j):
                    weigh(j - 1, 1 - par)

            bias_tile(0, 0)
            low_tile(0, 0)
            low_tile(1, 1)
            dve.wait_ge(meta_in, 16)
            tiles(dve, body)
            weigh(TILES - 1, (TILES - 1) % 2)

        @block.tensor
        def _(pe):
            def mm(o, a, b, start, stop, **kw):
                return nc.tensor.matmul(o, a, b, start=start, stop=stop, **kw)

            def turn_xh(b):
                pe.wait_ge(xh_ready, b + 1)
                if not first(b, 3):
                    pe.wait_ge(oT_ready, b - 2)
                for c in range(DC):
                    ins = nc.tensor.transpose(psM[:, c * T:(c + 1) * T], xh[:, c * P:(c + 1) * P], ident)
                ins.then_inc(xhT_ps, 1)

            def project(b, par):
                pe.wait_ge(xhT_ready, b + 1)
                pe.wait_ge(ld_ctx[par], 32 * (b // 2 + 1) if isinstance(b, int) else 16 * (b - par) + 32)
                if not first(b):
                    pe.wait_ge(qk_ready, b)
                for k, src in ((0, xhT), (1, cT[par])):
                    for o in range(DC):
                        for c in range(DC):
                            ins = mm(psQK[:, (k * DC + o) * T:(k * DC + o + 1) * T], wproj_at(k, c)[:, o * P:(o + 1) * P],
                                     src[:, c * T:(c + 1) * T], c == 0, c == DC - 1)
                ins.then_inc(qk_ps, 1)
                if not first(b, 3):
                    pe.wait_ge(x1_ready, b - 2)
                if not first(b):
                    pe.wait_ge(v_ready, b)
                for c in range(DC):
                    ins = mm(psVY[:, 0:D], cT[par][:, c * T:(c + 1) * T], wproj_at(2, c), c == 0, c == DC - 1)
                ins.then_inc(v_ps, 1)

            def scores(n, r, par, b):
                if r == 0:
                    pe.wait_ge(qk_ready, b + 1)
                if not (first(b) and r < 2):
                    pe.wait_ge(biased, n - 1)
                rows = slice(32 * r, 32 * r + 32)
                for j in range(HR):
                    c, e = j // 2, j % 2
                    ins = mm(psS[r % 2][:, j * T:(j + 1) * T], qT[par][rows, c * T:(c + 1) * T],
                             kz[par][rows, (e * DC + c) * T:(e * DC + c + 1) * T], True, True)
                ins.then_inc(s_ps, 1)

            def turn_probs(n, r, b):
                pe.wait_ge(probs, n + 1)
                if not (first(b) and r < 2):
                    pe.wait_ge(pt_lo, n - 1)
                for j in range(HR):
                    ins = nc.tensor.transpose(psT[r % 2][:, j * T:(j + 1) * T], sc[r][:, j * T:(j + 1) * T], ident)
                ins.then_inc(pt_ps, 1)

            def weigh_values(n, r, par, b):
                pe.wait_ge(pt_lo, n + 1)
                if r == 0:
                    pe.wait_ge(v_ready, b + 1)
                    if not first(b):
                        pe.wait_ge(o_ready, b)
                k = r % 2
                for j in range(HR):
                    h = head(r, j)
                    cols_ = slice(h * HD, (h + 1) * HD)
                    pj = slice(j * T, (j + 1) * T)
                    mm(psO[:, cols_], pth[k][:, pj], vh[par][:, cols_], True, False)
                    mm(psO[:, cols_], pth[k][:, pj], vl[par][:, cols_], False, False)
                    ins = mm(psO[:, cols_], ptl[k][:, pj], vh[par][:, cols_], False, True)
                ins.then_inc(pv, 1)

            def turn_o(b):
                pe.wait_ge(o_ready, b + 1)
                if not last(b):
                    pe.wait_ge(xhT_ready, b + 3) if not (isinstance(b, int) and b + 3 > B) else None
                for c in range(DC):
                    ins = nc.tensor.transpose(psM[:, c * T:(c + 1) * T], on[:, c * P:(c + 1) * P], ident)
                ins.then_inc(oT_ps, 1)

            def project_o(b):
                pe.wait_ge(oT_ready, b + 1)
                if not (isinstance(b, int) and b + 3 > B):
                    pe.wait_ge(v_ready, b + 3)
                for c in range(DC):
                    ins = mm(psVY[:, D:2 * D], oT[:, c * T:(c + 1) * T], wproj_at(3, c), c == 0, c == DC - 1)
                ins.then_inc(y_ps, 1)

            def seq(b, par):
                for r in range(R):
                    n = R * b + r
                    if r < R - 1:
                        scores(n + 1, r + 1, par, b)
                    elif not last(b):
                        scores(n + 1, 0, 1 - par, b + 1)
                    if r == 3 and not first(b):
                        project_o(b - 1)
                    if r == 1 and not last(b):
                        project(b + 1, 1 - par)
                    turn_probs(n, r, b)
                    if r >= 1:
                        weigh_values(n - 1, r - 1, par, b)
                    elif not first(b):
                        weigh_values(n - 1, R - 1, 1 - par, b - 1)
                    if r == 0 and not last(b):
                        turn_xh(b + 1)
                    if r == 2 and not first(b):
                        turn_o(b - 1)

            pe.wait_ge(ld_par, 48)
            turn_xh(0)
            pe.wait_ge(ld_wp, 16)
            project(0, 0)
            scores(0, 0, 0, 0)
            pairs(pe, seq)
            weigh_values(STEPS - 1, R - 1, 1, B - 1)
            turn_o(B - 1)
            project_o(B - 1)

            def turn2(b, par):
                pe.wait_ge(xh2_ready, b + 1)
                if not first(b, 2):
                    pe.wait_ge(x2_lo, b - 1)
                for c in range(DC):
                    ins = nc.tensor.transpose(bank[6 + par][:, c * T:(c + 1) * T], hbuf[:, par, c * P:(c + 1) * P], ident)
                ins.then_inc(x2T_ps, 1)

            pe.wait_ge(x1_ready, B)
            turn2(0, 0)
            turn2(1, 1)
            with pe.Fori(1, PAIRS) as i:
                turn2(2 * i, 0)
                turn2(2 * i + 1, 1)
            pe.wait_ge(x2_lo, B)
            for b in range(B):
                for c in range(DC):
                    for p in range(4):
                        xk = xT2[:, (p % 2) * DC * N + c * N + b * T:(p % 2) * DC * N + c * N + (b + 1) * T]
                        ins = mm(bank[4][:, b * E:(b + 1) * E], xk, gwhl[:, p // 2, c, :],
                                 c == 0 and p == 0, c == DC - 1 and p == 3)
            ins.then_inc(gate_ps, 1)
            pe.wait_ge(sel_ready, 1)
            sel = selm.rearrange("p b e -> p (b e)")
            mm(bank[5][:, 0:B * E], upb[:], sel, True, True)
            mm(bank[5][:, B * E:2 * B * E], oneb[:], sel, True, True).then_inc(rank_ps, 1)

            def w_up(base, part, c, j):
                return W[:, bass.ds(base + (W1L if part else W1H) + c * HID + j * P, P)]

            def w_down(base, part, j):
                return W[:, bass.ds(base + (W2L if part else W2H) + j * D, D)]

            def shared_up(g, j):
                if not (first(g) and j < 2):
                    pe.wait_ge(sg_ready, HC * g + j - 1)
                n = 0
                for wpart, xpart in ((0, 0), (1, 0), (0, 1)):
                    for c in range(DC):
                        ins = mm(bank[j % 2][:], w_up(0, wpart, c, j),
                                 xT2[:, bass.ds(xpart * DC * N + c * N + g * 512, 512)], n == 0, n == 5)
                        n += 1
                ins.then_inc(su_ps, 1)

            def shared_down(g, y, j):
                pe.wait_ge(sh_ready, HC * g + j + 1)
                if j == 0 and not first(g, 2):
                    pe.wait_ge(acc_half, 4 * (g - 1))
                n = 0
                for hpart, wpart in ((0, 0), (0, 1), (1, 0)):
                    for t in range(4):
                        ins = mm(bank[2 + 2 * y + t // 2][:, (t % 2) * D:(t % 2 + 1) * D],
                                 hsplit[:, j % 2, hpart, t * P:(t + 1) * P], w_down(0, wpart, j),
                                 j == 0 and n == 0 and t % 2 == 0, j == HC - 1 and n == 2, skip_group_check=True)
                    n += 1
                ins.then_inc(sd_used, 1)
                return ins

            pe.wait_ge(routed, 1)
            pe.wait_ge(converted, 4)

            def shared_group(g, y):
                shared_up(g, 0)
                for j in range(1, HC):
                    shared_up(g, j)
                    shared_down(g, y, j - 1)
                shared_down(g, y, HC - 1)
                nc.tensor.matmul(bank[7][:, 0:1], oneb[:], oneb[:, 0:1], start=True, stop=True).then_inc(sy_ps, 1)

            shared_group(0, 0)
            shared_group(1, 1)
            with pe.Fori(1, GROUPS // 2) as i:
                shared_group(2 * i, 0)
                shared_group(2 * i + 1, 1)

            def turn_tile(j, par):
                pe.wait_ge(xs_in[par], 16 * (j // 2) + 16 if isinstance(j, int) else 8 * (j - par) + 16)
                if not first(j, 2):
                    pe.wait_ge(xs_lo, j - 1)
                for t in range(TH):
                    for c in range(DC):
                        ins = nc.tensor.transpose(bank[6 + par][:, (c * TH + t) * P:(c * TH + t + 1) * P],
                                                  xs[par][:, (t * DC + c) * P:(t * DC + c + 1) * P], ident)
                ins.then_inc(xsT_ps, 1)

            def base_of(j):
                e = pe.value_load(tei[0:1, bass.ds(j, 1)], min_val=0, max_val=E - 1)
                return (e + 1) * WS

            def up_tile(j, par):
                base = base_of(j)
                pe.wait_ge(xs_lo, j + 1)
                for q in range(4):
                    if not first(j):
                        pe.wait_ge(g_ready, 4 * (j - 1) + q + 1)
                    for h in range(2):
                        n = 0
                        for wpart, xpart in ((0, 0), (0, 1), (1, 0)):
                            for c in range(DC):
                                ins = mm(bank[q][:, h * TR:(h + 1) * TR], w_up(base, wpart, c, 2 * q + h),
                                         xsT[par][:, (xpart * DC + c) * TR:(xpart * DC + c + 1) * TR], n == 0, n == 5)
                                n += 1
                    ins.then_inc(up_ps, 1)

            def down_tile(j, par):
                base = base_of(j)
                if not first(j, 2):
                    pe.wait_ge(y_ready, j - 1)
                y = [bank[4 + par][:, t * D:(t + 1) * D] for t in range(TH)]
                for t in range(TH):
                    mm(y[t], selb[:], b2hl[:, bass.ds((base - WS) // (WS // D), D)], t == 0, False, skip_group_check=True)
                for c in range(HC):
                    if c % 2 == 0:
                        pe.wait_ge(h_ready, 4 * j + c // 2 + 1)
                    for hpart, wpart in ((0, 0), (1, 0), (0, 1)):
                        for t in range(TH):
                            at = (hpart * HC + c) * TR + t * P
                            ins = mm(y[t], hs[par][:, at:at + P], w_down(base, wpart, c),
                                     False, c == HC - 1 and wpart == 1, skip_group_check=True)
                ins.then_inc(down_ps, 1)

            turn_tile(0, 0)
            turn_tile(1, 1)

            def body(j, par, more):
                up_tile(j, par)
                if more == 2:
                    turn_tile(j + 2, par)
                if not first(j):
                    down_tile(j - 1, 1 - par)

            pe.wait_ge(converted, 4 * (1 + E))
            pe.wait_ge(b2_done, 1)
            tiles(pe, body)
            down_tile(TILES - 1, (TILES - 1) % 2)


def kernel(**inputs):
    import numpy as np
    import concourse.bacc as bacc
    from concourse.bass_utils import run_bass_kernel_spmd

    def a(name):
        return np.asarray(inputs[name], order="C")

    def chunks(v):
        return v.reshape(-1, P).T

    f = np.float32
    x = a("x")
    ctxT = np.ascontiguousarray(a("ctx_1024").reshape(N, D).T.reshape(DC, P, N))
    frac = np.ascontiguousarray(a("fside_BxS2_0").reshape(1, N))
    wproj = np.stack([a(f"L0_xattn_W{k}").T for k in "qkvo"])
    p = np.arange(P)
    consts = np.concatenate([
        np.eye(P), p[:, None] < p[None, :],
        np.stack([p % 32 < HD, p % 32 >= HD, p == 0, p == 1, p < 2], 1),
        np.tile(np.arange(E), (P, 1)), p[:, None] + T * np.arange(B)[None], N + p[:, None] + P * np.arange(TH)[None],
        np.tile(np.arange(TILES), (P, 1))], axis=1).astype(f)
    cols = np.concatenate([
        chunks(a("L0_xattn_bq")), chunks(a("L0_xattn_bk")), chunks(a("L0_xattn_bv")),
        a("fside_BxS2_0").T, chunks(a("L0_ffn_bs1")),
        a("L0_ffn_b1").reshape(E, HC, P).transpose(2, 0, 1).reshape(P, E * HC),
        a("L0_ffn_gate_w").reshape(DC, P, E).transpose(1, 0, 2).reshape(P, DC * E)], axis=1)
    rows = np.concatenate([
        a("L0_xattn_alpha_pos"), a("L0_xattn_alpha_neg"), a("L0_xattn_gamma").reshape(1),
        a("L0_xattn_delta").reshape(1), a("g_xattn").reshape(1), a("g_ffn").reshape(1),
        a("L0_ffn_gate_b"), a("L0_xattn_bo"), a("L0_ffn_bs2")])[None]
    b2 = a("L0_ffn_b2").reshape(1, E * D)
    w1 = np.concatenate([a("L0_ffn_ws1")[None], a("L0_ffn_w1")]).reshape((1 + E) * D, HID)
    w2 = np.concatenate([a("L0_ffn_ws2")[None], a("L0_ffn_w2")]).reshape((1 + E) * HID, D)

    nc = bacc.Bacc("TRN2", target_bir_lowering=False, num_devices=1)
    arrays, args = {}, []
    for name, v in dict(x=x, ctxT=ctxT, frac=frac, wproj=wproj, consts=consts, cols=cols, rows=rows,
                        b2=b2, w1=w1, w2=w2).items():
        arrays[name] = np.ascontiguousarray(v)
        args.append(nc.dram_tensor(name, v.shape, mybir.dt.from_np(v.dtype), kind="ExternalInput").ap())
    xs_dram = nc.dram_tensor("xs_dram", (TILES * TR, ROW), mybir.dt.float32).ap()
    out = nc.dram_tensor("out", (N + TR, D), mybir.dt.float32, kind="ExternalOutput").ap()
    build(nc, *args, xs_dram, out)
    r = run_bass_kernel_spmd(nc, [arrays], core_ids=[0])
    return r.results[0]["out"][:N].reshape(B, T, D)
```

```python
import concourse.bass as bass
from concourse import mybir
from contextlib import ExitStack

P = 128
B, T, D = 16, 128, 256
H, HD = 16, 16
E, HID = 8, 1024
N = B * T
DC = D // P
HC = HID // P
R = 4
HR = H // R
PAIRS = B // 2
TOPK = 2
TR = 256
TH = TR // P
TILES = N * TOPK // TR + E - 1
GROUPS = N // 512
CLAMP = 0.2
EPS = 1e-5
ROW = D + 2

WS = 2 * 2 * DC * HID
W1H, W1L, W2H, W2L = (k * DC * HID for k in range(4))
EARLY = 4
PIECES = 4 * (1 + E)
NOW = 4 * EARLY
MIXED = (3,)
MOVED_BY_VECTOR = (1,)
DEEP = 3
PAD_TILES = (TILES - 1) // (PAIRS - 1)
PADS = 16 * TH * (PAIRS + 1)
POOL_PIECES_AT = (1, 3, 4, 6, 7)
VECTOR_PIECES = range(PIECES - 12, PIECES - 4)
HIGHS_AT = (10, 11, 13, 15, 18, 20, 22, 23)
LOWS_AT = (11, 12, 14, 16, 19, 21, 23, 24)
LAST_HIGHS_AT = (28, 30)
ROWS_AT = (10, 11, 12, 13, 14, 15, 16, 18, 19, 20, 21, 22)
POOL_SPLITS = HC

C_ID, C_UP = 0, P
C_EVEN, C_ODD = 2 * P, 2 * P + 1
C_IOTA = 2 * P + 2
C_TOK = C_IOTA + E
C_PAD = C_TOK + B
C_TILE = C_PAD + TH
C_N = C_TILE + TILES
K_BQ, K_BK, K_BV, K_FR = 0, DC, 2 * DC, 3 * DC
K_BS1 = K_FR + B
K_B1 = K_BS1 + HC
K_GW = K_B1 + E * HC
K_N = K_GW + DC * E
V_AP, V_AN, V_GAMMA, V_DELTA, V_GX, V_GF = 0, H, 2 * H, 2 * H + 1, 2 * H + 2, 2 * H + 3
V_GB = 2 * H + 4
V_BO = V_GB + E
V_BS2 = V_BO + D
V_N = V_BS2 + D


def head(r, j):
    return 8 * (j // 2) + 2 * r + j % 2


def build(nc, x, ctxT, frac, wproj, consts, cols, rows, b2, wts, xs_dram, out):
    fp32, bf16 = mybir.dt.float32, mybir.dt.bfloat16
    i32, u32 = mybir.dt.int32, mybir.dt.uint32
    ALU, ACT, AX = mybir.AluOpType, mybir.ActivationFunctionType, mybir.AxisListType

    with ExitStack() as ctx:
        def sb(name, shape, dt=fp32):
            return ctx.enter_context(nc.sbuf_tensor(name, shape, dt))

        def sem(name):
            return ctx.enter_context(nc.semaphore(name))

        W = sb("W", [P, (1 + E) * WS], bf16)
        xres = sb("xres", [P, (B - 4 + E) * D])
        xT2 = sb("xT2", [P, 2 * DC * N], bf16)
        stage = sb("stage", [P, 2 * HID])
        hbuf = sb("hbuf", [P, DEEP, 512])
        hsplit = sb("hsplit", [P, DEEP, 2, 512], bf16)
        cst = sb("cst", [P, C_N])
        col = sb("col", [P, K_N])
        row = sb("row", [P, V_N])
        upb = sb("upb", [P, P], bf16)
        oneb = sb("oneb", [P, P], bf16)
        gwhl = sb("gwhl", [P, 2, DC, E], bf16)
        ident = cst[:, C_ID:C_ID + P]

        top = [EARLY * WS]

        def under(n, dt=fp32):
            size = n * (2 if dt == fp32 else 1)
            at = top[0]
            top[0] += size
            assert top[0] <= (1 + E) * WS
            v = W[:, at:at + size]
            return v.bitcast(fp32) if dt == fp32 else v

        sc = [under(HR * T) for _ in range(R)]
        pb = [under(HR * T) for _ in range(R)]
        pbn = under(HR * T)
        pT = [under(HR * T) for _ in range(2)]
        qT = [under(DC * T) for _ in range(2)]
        kz = [under(2 * DC * T) for _ in range(2)]
        vf = [under(D) for _ in range(2)]
        cT = [under(DC * T) for _ in range(2)]
        xh = under(D)
        xhT = under(DC * T)
        on = under(D)
        oT = under(DC * T)
        fr = [under(T) for _ in range(2)]
        dneg = [under(T) for _ in range(2)]
        dd = under(T)
        dpos = under(T)
        wp = under(4 * DC * D)
        bo_t = under(D)

        def wproj_at(k, c):
            return wp[:, (k * DC + c) * D:(k * DC + c + 1) * D]

        GD = 4 * D
        xs = [xres[:, k * TH * D:(k + 1) * TH * D] for k in range(2)]
        ysb = [[xres[:, GD + (TH * k + t) * D:GD + (TH * k + t + 1) * D] for t in range(TH)] for k in range(2)]
        xsT = [xres[:, 2 * GD + k * DC * TR:2 * GD + (k + 1) * DC * TR].bitcast(bf16) for k in range(2)]
        b2f = xres[:, 3 * GD:3 * GD + E * D]
        hs = [xT2[:, k * 2 * HC * TR:(k + 1) * 2 * HC * TR] for k in range(2)]

        st6 = sb("st6", [P, B, 6])
        mv1 = sb("mv1", [P, B, 2])
        mv2 = sb("mv2", [P, B, 2])
        rstd1 = sb("rstd1", [P, B])
        rstd2 = sb("rstd2", [P, B])
        mhalf = sb("mhalf", [P, B])
        mn = sb("mn", [P, 2, H])
        sm = sb("sm", [P, 2, H])
        rs = sb("rs", [P, H])
        tgx = sb("tgx", [P, 1])
        tgf = sb("tgf", [P, 1])
        gs = sb("gs", [P, 1])
        bqs = sb("bqs", [P, DC])
        bkm = sb("bkm", [P, 2, DC])
        apd = sb("apd", [P, H])
        and_ = sb("and_", [P, H])
        bs2t = row[:, V_BS2:V_BS2 + D]
        top = [E * WS]
        lg, mx8, ix8f, oh0, oh1, ca0, ca1, offs = (
            under(B * E).rearrange("p (b e) -> p b e", e=E) for k in range(8))
        ix8 = ix8f.bitcast(u32)
        oh, ca = [oh0, oh1], [ca0, ca1]
        rank = under(2 * B * E).rearrange("p (k b e) -> p k b e", k=2, e=E)
        tcmp = under(TILES * E).rearrange("p (j e) -> p j e", e=E)
        selm = under(B * E, bf16).rearrange("p (b e) -> p b e", e=E)
        pay = under(4 * TOPK * ROW).rearrange("p (n k d) -> p n k d", n=4, k=TOPK)
        ixf = sb("ixf", [P, B, TOPK])
        wt = sb("wt", [P, B, TOPK])
        wid = sb("wid", [P, B, TOPK, 2])
        ed = sb("ed", [P, B])
        meta = sb("meta", [P, TILES * TH, 2])
        posf = sb("posf", [P, TOPK, B])
        posu = sb("posu", [P, TOPK, B], u32)
        place = sb("place", [P, 4, TOPK], u32)
        te_i = sb("te_i", [P, E], i32)
        te = [sb(f"te{k}", [P, E]) for k in range(3)]
        tef = sb("tef", [P, TILES])
        tei = sb("tei", [P, TILES], i32)
        b1t = sb("b1t", [P, 2, HC])
        idu = sb("idu", [P, 2, TH], u32)
        padt = hbuf[:].rearrange("p a n -> p (a n)")[:, 0:TH * ROW].rearrange("p (k d) -> p k d", k=TH)

        bank = [ctx.enter_context(nc.psum_tensor(f"bank{k}", [P, 512], fp32)) for k in range(8)]
        psS, psT, psQK, psO, psM, psVY = bank[0:2], bank[2:4], bank[4], bank[5], bank[6], bank[7]

        ld_par, ld_b2 = sem("ld_par"), sem("ld_b2")
        ld_wp = [sem(f"ld_wp{k}") for k in range(4)]
        ld_x = [sem(f"ld_x{k}") for k in range(4)]
        ld_ctx = [sem(f"ld_ctx{k}") for k in range(2)]
        ld_st = [sem(f"ld_st{k}") for k in range(2)]
        pad_ready, pad_written = sem("pad_ready"), sem("pad_written")
        setup_act, setup_dve, setup_pool = sem("setup_act"), sem("setup_dve"), sem("setup_pool")
        ln1_stat, ln1_rstd = sem("ln1_stat"), sem("ln1_rstd")
        converted, converted_v, biased_y = sem("converted"), sem("converted_v"), sem("biased_y")
        xh_ready, xhT_ps, xhT_ready = sem("xh_ready"), sem("xhT_ps"), sem("xhT_ready")
        q_ps, q_ready, k_ps, k_ready = sem("q_ps"), sem("q_ready"), sem("k_ps"), sem("k_ready")
        v_ps, v_ready, pb_parts = sem("v_ps"), sem("v_ready"), sem("pb_parts")
        d_ready, pb_ready, xb_ready = sem("d_ready"), sem("pb_ready"), sem("xb_ready")
        s_ps, biased, scored, probs = sem("s_ps"), sem("biased"), sem("scored"), sem("probs")
        pt_ps, pt_dve, pt_act, pv = sem("pt_ps"), sem("pt_dve"), sem("pt_act"), sem("pv")
        o_ready, oT_ps, oT_ready, y_ps, x1_ready = (sem("o_ready"), sem("oT_ps"), sem("oT_ready"),
                                                    sem("y_ps"), sem("x1_ready"))
        dve_own, pool_own = sem("dve_own"), sem("pool_own")
        ln2_stat, ln2_rstd = sem("ln2_stat"), sem("ln2_rstd")
        xh2_ready, x2T_ps, x2_hi, x2_lo, gate_ps = (sem("xh2_ready"), sem("x2T_ps"), sem("x2_hi"),
                                                    sem("x2_lo"), sem("gate_ps"))
        wd_ready, we_ready, sel_ready, rank_ps, routed = (sem("wd_ready"), sem("we_ready"), sem("sel_ready"),
                                                        sem("rank_ps"), sem("routed"))
        pay_ready = sem("pay_ready")
        dispatched = [sem(f"dispatched{k}") for k in range(4)]
        su_ps, sg_ready, sd_used, acc_ready = sem("su_ps"), sem("sg_ready"), sem("sd_used"), sem("acc_ready")
        sh_ready = [sem("sh_pool"), sem("sh_dve")]
        ranks_read = sem("ranks_read")
        out_written = [sem(f"out_written{g}") for g in range(GROUPS)]
        xs_in = [sem(f"xs_in{k}") for k in range(2)]
        xsT_ps, xs_hi, xs_lo, meta_in = sem("xsT_ps"), sem("xs_hi"), sem("xs_lo"), sem("meta_in")
        b1_ready, up_ps, g_ready, h_ready, down_ps, y_ready = (sem("b1_ready"), sem("up_ps"), sem("g_ready"),
                                                               sem("h_ready"), sem("down_ps"), sem("y_ready"))
        added = [sem(f"added{k}") for k in range(2)]
        dpos_done, dneg_done, conv_hi = sem("dpos_done"), sem("dneg_done"), sem("conv_hi")
        rs_done, st_done, sh_hi, h_hi, acc_half = (sem("rs_done"), sem("st_done"),
                                                          sem("sh_hi"), sem("h_hi"), sem("acc_half"))

        def pairs(eng, body):
            body(0, 0)
            body(1, 1)
            with eng.Fori(1, PAIRS - 1) as i:
                body(2 * i, 0)
                body(2 * i + 1, 1)
            body(B - 2, 0)
            body(B - 1, 1)

        passed = {}

        def wait_alone(eng, name, s, value):
            if name not in passed:
                passed[name] = sem(f"passed_{name}")
            eng.wait_ge(s, value)
            eng.sem_inc(passed[name], 1)

        def tiles(eng, body):
            body(0, 0, 2)
            body(1, 1, 2)
            with eng.Fori(1, TILES // 2 - 1) as i:
                body(2 * i, 0, 2)
                body(2 * i + 1, 1, 2)
            for j in range(TILES - 3, TILES):
                body(j, j % 2, min(2, TILES - 1 - j))

        LN2 = ((0, B - 4), (B - 4, B))

        def within(b):
            return not isinstance(b, int) or b < B

        def biased_through(b, r):
            return (R - len(MIXED)) * b + sum(k not in MIXED for k in range(r + 1))

        def scores_read(eng, b, r):
            if r in MIXED:
                eng.wait_ge(scored, R * b + r + 1)
            else:
                eng.wait_ge(biased, biased_through(b, r))

        def moved(eng, b, r):
            by_vector = [k in MOVED_BY_VECTOR for k in range(R)]
            count = sum(k == by_vector[r] for k in by_vector) * b + sum(k == by_vector[r] for k in by_vector[:r + 1])
            eng.wait_ge(pt_dve if by_vector[r] else pt_act, count)

        def split_ready(eng, m):
            if m < POOL_SPLITS:
                eng.wait_ge(sh_ready[0], m + 1)
            else:
                eng.wait_ge(sh_ready[1], m - POOL_SPLITS + 1)

        def after(b, r, k):
            return b + (r + k) // R, (r + k) % R

        def piece_converted(eng, m):
            if m in VECTOR_PIECES:
                eng.wait_ge(converted_v, m - VECTOR_PIECES[0] + 1)
            else:
                eng.wait_ge(converted, m + 1 - (len(VECTOR_PIECES) if m > VECTOR_PIECES[0] else 0))

        def piece_at(i, k):
            return i * 2 * DC * HID + k * HID

        def first(b, n=1):
            return isinstance(b, int) and b < n

        block = ctx.enter_context(nc.Block())

        @block.sync
        def _(sp):
            def load_x(k):
                sp.dma_start(xres[:, k * 4 * D:(k + 1) * 4 * D].rearrange("p (b d) -> p b d", d=D),
                             x[4 * k:4 * k + 4].rearrange("b p d -> p b d")).then_inc(ld_x[k], 16)

            def load_proj(k):
                sp.dma_start(wp[:, k * DC * D:(k + 1) * DC * D].rearrange("p (c d) -> p c d", d=D),
                             wproj[k].rearrange("(c p) d -> p c d", p=P)).then_inc(ld_wp[k], 16)

            def load_seq(b, par):
                if not first(b, 2):
                    sp.wait_ge(v_ps, b - 1)
                    sp.wait_ge(d_ready, b - 1)
                sp.dma_start(cT[par].rearrange("p (c t) -> p c t", c=DC),
                             ctxT[:, :, bass.ds(b * T, T)].rearrange("c p t -> p c t")).then_inc(ld_ctx[par], 16)
                sp.dma_start(fr[par], frac[:, bass.ds(b * T, T)].to_broadcast([P, T])).then_inc(ld_ctx[par], 16)

            load_x(0)
            sp.dma_start(cst[:], consts).then_inc(ld_par, 16)
            load_seq(0, 0)
            load_proj(1)
            sp.dma_start(col[:], cols).then_inc(ld_par, 16)
            sp.dma_start(row[:], rows.to_broadcast([P, V_N])).then_inc(ld_par, 16)
            load_proj(2)
            load_proj(0)
            load_seq(1, 1)
            load_x(1)
            load_proj(3)
            load_x(2)
            load_x(3)
            def load_piece(i, k):
                if not isinstance(i, int):
                    sp.wait_ge(converted, 2 * i + k - 1)
                elif i > 0:
                    piece_converted(sp, 2 * i + k - 2)
                sp.dma_start(stage[:, k * HID:(k + 1) * HID], wts[bass.ds((2 * i + k) * P, P), :]).then_inc(ld_st[k], 16)

            def write_pads(j, n, ks=range(TH)):
                for k in ks:
                    sp.dma_start(xs_dram.rearrange("(j k p) d -> k p j d", k=TH, p=P)[k][:, bass.ds(j, n), :],
                                 padt[:, k:k + 1, :].to_broadcast([P, n, ROW])).then_inc(pad_written, 16)

            load_piece(0, 0)
            load_piece(0, 1)
            sp.wait_ge(pad_ready, 1)
            with sp.Fori(1, PAIRS) as i:
                for k in range(2):
                    load_seq(2 * i + k, k)
                    load_piece(i, k)
                    write_pads((i - 1) * PAD_TILES, PAD_TILES, (k,))
            write_pads((PAIRS - 1) * PAD_TILES, TILES - (PAIRS - 1) * PAD_TILES)
            for k in range(TH):
                sp.dma_start(out[N + k * P:N + (k + 1) * P, :], padt[:, 0, 0:D]).then_inc(pad_written, 16)
            load_piece(NOW // 2, 0)
            load_piece(NOW // 2, 1)
            load_piece(NOW // 2 + 1, 0)
            load_piece(NOW // 2 + 1, 1)
            for i in range(NOW // 2 + 2, PIECES // 2 - 1):
                load_piece(i, 0)
                load_piece(i, 1)

            def store_group(g):
                sp.wait_ge(acc_ready, g + 1)
                sp.dma_start(out[g * 512:(g + 1) * 512, :].rearrange("(t p) d -> p t d", p=P),
                             xres[:, g * GD:(g + 1) * GD].rearrange("p (t d) -> p t d", d=D)).then_inc(out_written[g], 16)

            store_group(0)
            store_group(1)

            for k in range(4):
                sp.wait_ge(dispatched[k], 16 * TOPK * B // 4)
            sp.wait_ge(out_written[0], 16)

            def load_tile(j, par):
                if not first(j, 2):
                    sp.wait_ge(xsT_ps, j - 1)
                sp.dma_start(xs[par].rearrange("p (t d) -> p t d", d=D),
                             xs_dram[bass.ds(j * TR, TR), 0:D].rearrange("(t p) d -> p t d", p=P)).then_inc(xs_in[par], 16)

            load_tile(0, 0)
            load_tile(1, 1)
            sp.dma_start(meta[:], xs_dram.rearrange("(j p) d -> p j d", p=P)[:, :, D:ROW]).then_inc(meta_in, 16)
            load_piece(PIECES // 2 - 1, 0)
            store_group(2)
            load_tile(2, 0)
            load_piece(PIECES // 2 - 1, 1)
            load_tile(3, 1)
            store_group(3)
            sp.wait_ge(out_written[3], 16)
            sp.dma_start(b2f, b2.to_broadcast([P, E * D])).then_inc(ld_b2, 16)
            with sp.Fori(2, TILES // 2) as i:
                load_tile(2 * i, 0)
                load_tile(2 * i + 1, 1)
            load_tile(TILES - 1, 0)

        @block.gpsimd
        def _(pool):
            own = [0]

            def link(ins):
                own[0] += 1
                ins.then_inc(pool_own, 1)
                pool.wait_ge(pool_own, own[0])

            def inverse_deviation(rstd, mv, lo, hi):
                link(nc.gpsimd.tensor_scalar(rstd[:, lo:hi], mv[:, lo:hi, 1], EPS, None, ALU.add))
                return nc.gpsimd.tensor_tensor(rstd[:, lo:hi], rstd[:, lo:hi], mhalf[:, lo:hi], ALU.pow)

            nc.gpsimd.memset(mhalf[:], -0.5).then_inc(pool_own, 1)
            nc.gpsimd.memset(padt, 0.0).then_inc(pool_own, 1)
            own[0] += 2
            pool.wait_ge(pool_own, own[0])
            pool.wait_ge(ln1_stat, 4)
            inverse_deviation(rstd1, mv1, 0, 4).then_inc(ln1_rstd, 1)
            pool.wait_ge(ld_par, 48)
            nc.gpsimd.tensor_copy(padt[:, :, D + 1:D + 2], cst[:, C_PAD:C_PAD + TH].rearrange("p (k o) -> p k o", o=1)).then_inc(pad_ready, 1)

            def over_keys(t, r):
                return t[:, HR * r:HR * (r + 1)].rearrange("p (j o) -> p j o", o=1).to_broadcast([P, HR, T])

            def over_heads(t):
                return t.rearrange("p (o t) -> p o t", o=1).to_broadcast([P, HR, T])

            def by_head(t):
                return t.rearrange("p (j t) -> p j t", j=HR)

            def seq(b, par):
                if isinstance(b, int):
                    pool.wait_ge(ld_ctx[par], 32 * (b // 2 + 1))
                else:
                    pool.wait_ge(ld_ctx[par], 16 * (b - par) + 32)
                if not first(b):
                    pool.wait_ge(pb_ready, R * b)
                nc.gpsimd.tensor_tensor(dd, fr[par], col[:, bass.ds(K_FR + b, 1)].to_broadcast([P, T]), ALU.subtract).then_inc(d_ready, 1)
                wait_alone(pool, "pool", d_ready, b + 1)
                if not first(b, 2):
                    wait_alone(pool, "pool", biased, biased_through(b - 2, R - 1))
                nc.gpsimd.tensor_scalar(dneg[par], dd, 0.0, -CLAMP, ALU.min, ALU.max).then_inc(dneg_done, 1)
                nc.gpsimd.tensor_scalar(dpos, dd, 0.0, CLAMP, ALU.max, ALU.min).then_inc(dpos_done, 1)
                wait_alone(pool, "pool", dpos_done, b + 1)
                for r in range(R):
                    if not first(b):
                        pool.wait_ge(scored, R * b + r - 3)
                    if r in MIXED:
                        nc.gpsimd.tensor_tensor(by_head(pb[r]), over_heads(dpos), over_keys(apd, r), ALU.mult).then_inc(pb_parts, 1)
                        wait_alone(pool, "pool", dneg_done, b + 1)
                        nc.gpsimd.tensor_tensor(by_head(pbn), over_heads(dneg[par]), over_keys(and_, r), ALU.mult).then_inc(pb_parts, 1)
                        pool.wait_ge(pb_parts, 2 * (len(MIXED) * b + MIXED.index(r) + 1))
                        nc.gpsimd.tensor_tensor(pb[r], pb[r], pbn, ALU.add).then_inc(pb_ready, 1)
                    else:
                        nc.gpsimd.tensor_tensor(by_head(pb[r]), over_heads(dpos), over_keys(apd, r), ALU.mult).then_inc(pb_ready, 1)
                pool.wait_ge(xh_ready, b + 1)
                xb = xres[:, bass.ds(b * D, D)]
                nc.gpsimd.tensor_tensor(xb, xb, bo_t, ALU.add).then_inc(xb_ready, 1)

            def piece_low(i, k):
                hi = W[:, bass.ds(piece_at(i, k), HID)]
                lo = W[:, bass.ds(piece_at(i, k) + DC * HID, HID)]
                pool.wait_ge(conv_hi, 2 * i + k + 1)
                nc.gpsimd.tensor_tensor(lo, stage[:, k * HID:(k + 1) * HID], hi, ALU.subtract).then_inc(converted, 1)

            pool.wait_ge(setup_act, 2)
            link(nc.gpsimd.tensor_scalar(bo_t, row[:, V_BO:V_BO + D], tgx[:, 0:1], None, ALU.mult))
            pool.wait_ge(setup_dve, 2)
            seq(0, 0)
            seq(1, 1)
            pool.wait_ge(ln1_stat, B)
            inverse_deviation(rstd1, mv1, 4, B).then_inc(ln1_rstd, 1)
            piece_low(0, 0)
            nc.gpsimd.tensor_scalar(bs2t, row[:, V_BS2:V_BS2 + D], tgf[:, 0:1], None, ALU.mult).then_inc(setup_pool, 1)
            with pool.Fori(1, PAIRS) as i:
                seq(2 * i, 0)
                piece_low(i - 1, 1)
                seq(2 * i + 1, 1)
                piece_low(i, 0)
            for lo, hi in LN2:
                pool.wait_ge(ln2_stat, hi)
                inverse_deviation(rstd2, mv2, lo, hi).then_inc(ln2_rstd, 1)
                if lo == 0:
                    piece_low(PAIRS - 1, 1)

            for m in range(NOW, NOW + 3):
                piece_low(m // 2, m % 2)

            for m in range(POOL_SPLITS):
                pool.wait_ge(sh_hi, m + 1)
                nc.gpsimd.tensor_tensor(hsplit[:, m % DEEP, 1, :], hbuf[:, m % DEEP, :], hsplit[:, m % DEEP, 0, :],
                                        ALU.subtract).then_inc(sh_ready[0], 1)
                if m in POOL_PIECES_AT:
                    q = NOW + 3 + POOL_PIECES_AT.index(m)
                    piece_low(q // 2, q % 2)

            pool.wait_ge(pad_written, PADS)
            for b in range(B):
                pool.wait_ge(pay_ready, b + 1)
                for k in range(TOPK):
                    nc.gpsimd.indirect_dma_start(
                        xs_dram, bass.IndirectOffsetOnAxis(place[:, b % 4, k:k + 1], axis=0),
                        pay[:, b % 4, k, :], None).then_inc(dispatched[b % 4], 16)
            for i in range(PIECES // 2 - 2, PIECES // 2):
                for k in range(2):
                    piece_low(i, k)

            for g in range(GROUPS):
                pool.wait_ge(out_written[g], 16)

            def add_tile(j, par):
                wait_alone(pool, "pool", y_ready, j + 1)
                for t in range(TH):
                    if t == 0 and not first(j):
                        for k in range(TH):
                            wait_alone(pool, "pool", added[k], 16 * j)
                    nc.gpsimd.indirect_dma_start(
                        out, bass.IndirectOffsetOnAxis(idu[:, par, t:t + 1], axis=0),
                        ysb[par][t], None, compute_op=ALU.add).then_inc(added[t], 16)

            add_tile(0, 0)
            add_tile(1, 1)
            with pool.Fori(1, TILES // 2) as i:
                add_tile(2 * i, 0)
                add_tile(2 * i + 1, 1)
            add_tile(TILES - 1, 0)
            for t in range(TH):
                pool.wait_ge(added[t], 16 * TILES)

        @block.scalar
        def _(act):
            act.wait_ge(ld_par, 48)
            nc.scalar.activation(tgx[:], row[:, V_GX:V_GX + 1], ACT.Tanh).then_inc(setup_act, 1)
            nc.scalar.activation(tgf[:], row[:, V_GF:V_GF + 1], ACT.Tanh).then_inc(setup_act, 1)
            act.wait_ge(setup_dve, 1)

            def move_xhT(b):
                act.wait_ge(xhT_ps, b + 1)
                if not first(b):
                    act.wait_ge(q_ps, b)
                nc.scalar.activation(xhT, psM[:, 0:DC * T], ACT.Copy).then_inc(xhT_ready, 1)

            def move_q(b, par):
                act.wait_ge(q_ps, b + 1)
                if not first(b, 2):
                    act.wait_ge(s_ps, R * (b - 1))
                for c in range(DC):
                    ins = nc.scalar.activation(qT[par][:, c * T:(c + 1) * T], psQK[:, c * T:(c + 1) * T], ACT.Identity,
                                               scale=gs[:, 0:1], bias=bqs[:, c:c + 1])
                ins.then_inc(q_ready, 1)

            def move_k(b, par, e):
                if e == 0:
                    act.wait_ge(k_ps, b + 1)
                    if not first(b, 2):
                        act.wait_ge(s_ps, R * (b - 1))
                for c in range(DC):
                    ins = nc.scalar.activation(
                        kz[par][:, (e * DC + c) * T:(e * DC + c + 1) * T],
                        psQK[:, (DC + c) * T:(DC + c + 1) * T], ACT.Identity,
                        scale=cst[:, C_EVEN + e:C_EVEN + e + 1], bias=bkm[:, e, c:c + 1])
                if e == 1:
                    ins.then_inc(k_ready, 1)

            def move_probs(b, r):
                if r in MOVED_BY_VECTOR:
                    return
                n = R * b + r
                act.wait_ge(pt_ps, n + 1)
                if not (first(b) and r < 2):
                    act.wait_ge(pv, n - 1)
                nc.scalar.activation(pT[r % 2], psT[r % 2][:], ACT.Copy).then_inc(pt_act, 1)

            def exps(n, r, par):
                act.wait_ge(scored, n + 1)
                for j in range(HR):
                    q = r * HR + j
                    ins = nc.scalar.activation(sc[r][:, j * T:(j + 1) * T], sc[r][:, j * T:(j + 1) * T], ACT.Exp,
                                               scale=-1.0, bias=mn[:, par, q:q + 1], accum_out=sm[:, par, q:q + 1])
                ins.then_inc(probs, 1)

            def move_oT(b):
                act.wait_ge(oT_ps, b + 1)
                if not first(b):
                    act.wait_ge(y_ps, b)
                for c in range(DC):
                    ins = nc.scalar.activation(oT[:, c * T:(c + 1) * T], psM[:, c * T:(c + 1) * T], ACT.Identity,
                                               bias=col[:, K_BV + c:K_BV + c + 1])
                ins.then_inc(oT_ready, 1)

            def piece_high(i, k):
                act.wait_ge(ld_st[k], 16 * i + 16)
                nc.scalar.activation(W[:, bass.ds(piece_at(i, k), HID)], stage[:, k * HID:(k + 1) * HID], ACT.Copy).then_inc(conv_hi, 1)

            def seq(b, par):
                for r in range(R):
                    n = R * b + r
                    if r == 0 and not first(b, 2):
                        act.wait_ge(o_ready, b - 1)
                    exps(n, r, par)
                    if r == 0 and within(b + 1):
                        move_k(b + 1, 1 - par, 1)
                        move_xhT(b + 1)
                    if r == 1 and within(b + 1):
                        move_q(b + 1, 1 - par)
                    if r == 3 and within(b + 2):
                        move_k(b + 2, par, 0)
                    if r == 3 and not first(b):
                        move_oT(b - 1)
                    if not (first(b) and r == 0):
                        move_probs(*after(b, r, -1))
                    if r == 2:
                        piece_high(b // 2 if isinstance(b, int) else (b - par) // 2, par)

            move_k(0, 0, 0)
            move_k(0, 0, 1)
            move_xhT(0)
            move_q(0, 0)
            move_k(1, 1, 0)
            pairs(act, seq)
            move_probs(B - 1, R - 1)

            def high2(i, k):
                act.wait_ge(x2T_ps, i + 1)
                nc.scalar.activation(xT2[:, 0:DC * N].rearrange("p (c n) -> p c n", c=DC)[:, :, bass.ds(i * 2 * T, 2 * T)],
                                     bank[k][:].rearrange("p (c t) -> p c t", c=DC), ACT.Copy).then_inc(x2_hi, 1)

            for i in range(PAIRS):
                if i == 1:
                    move_oT(B - 1)
                high2(i, i % 3)
                if i == 4:
                    act.wait_ge(x1_ready, B)
                if i in (4, 5, PAIRS - 1):
                    m = NOW + (4, 5, PAIRS - 1).index(i)
                    piece_high(m // 2, m % 2)

            for m in range(HC * GROUPS):
                c = m % HC
                act.wait_ge(su_ps, m + 1)
                if m >= DEEP:
                    split_ready(act, m - DEEP)
                nc.scalar.activation(hbuf[:, m % DEEP, :], bank[(0, 1, 7)[m % DEEP]][:], ACT.Gelu,
                                     bias=col[:, K_BS1 + c:K_BS1 + c + 1]).then_inc(sg_ready, 1)
                if m == 3:
                    act.wait_ge(wd_ready, 1)
                    nc.scalar.activation(ed[:], ed[:], ACT.Exp).then_inc(we_ready, 1)
                act.wait_ge(sg_ready, m + 1)
                if m >= DEEP:
                    act.wait_ge(sd_used, m - DEEP + 1)
                nc.scalar.activation(hsplit[:, m % DEEP, 0, :], hbuf[:, m % DEEP, :], ACT.Copy).then_inc(sh_hi, 1)
                if m in POOL_PIECES_AT:
                    q = NOW + 3 + POOL_PIECES_AT.index(m)
                    piece_high(q // 2, q % 2)
                if m in LAST_HIGHS_AT:
                    if m == LAST_HIGHS_AT[0]:
                        for k in range(4):
                            act.wait_ge(dispatched[k], 16 * TOPK * B // 4)
                    piece_high(PIECES // 2 - 2, LAST_HIGHS_AT.index(m))
                if m in HIGHS_AT:
                    q = VECTOR_PIECES[HIGHS_AT.index(m)]
                    piece_high(q // 2, q % 2)

            def high_tile(j, par):
                act.wait_ge(xsT_ps, j + 1)
                if not first(j, 2):
                    act.wait_ge(up_ps, 4 * (j - 1))
                nc.scalar.activation(xsT[par][:, 0:DC * TR], bank[6 + par][:, 0:DC * TR], ACT.Copy).then_inc(xs_hi, 1)

            def gelu_tile(j, par):
                act.wait_ge(b1_ready, j + 1)
                for q in range(4):
                    act.wait_ge(up_ps, 4 * j + q + 1)
                    if not (first(j) and q < 2):
                        act.wait_ge(h_ready, 4 * j + q - 1)
                    for c in range(2):
                        ins = nc.scalar.activation(hbuf[:, q % 2, c * TR:(c + 1) * TR], bank[q][:, c * TR:(c + 1) * TR],
                                                   ACT.Gelu, bias=b1t[:, par, 2 * q + c:2 * q + c + 1])
                    ins.then_inc(g_ready, 1)

            def body(j, par, more):
                gelu_tile(j, par)
                if more == 2:
                    high_tile(j + 2, par)

            act.wait_ge(out_written[2], 16)
            high_tile(0, 0)
            high_tile(1, 1)
            piece_high(PIECES // 2 - 1, 0)
            piece_high(PIECES // 2 - 1, 1)
            tiles(act, body)

        @block.vector
        def _(dve):
            own = [0]

            def link(ins):
                own[0] += 1
                ins.then_inc(dve_own, 1)
                dve.wait_ge(dve_own, own[0])

            def stats1(b):
                if b % 4 == 0:
                    dve.wait_ge(ld_x[b // 4], 16)
                link(nc.vector.bn_stats(st6[:, b, :], xres[:, b * D:(b + 1) * D]))
                nc.vector.bn_aggr(mv1[:, b, :], st6[:, b, :]).then_inc(ln1_stat, 1)

            def norm1(b):
                if isinstance(b, int) and b < 4:
                    dve.wait_ge(ln1_rstd, 1 if b < 3 else 2)
                if not first(b):
                    dve.wait_ge(xhT_ps, b)
                nc.vector.tensor_scalar(xh, xres[:, bass.ds(b * D, D)], mv1[:, bass.ds(b, 1), 0], rstd1[:, bass.ds(b, 1)],
                                        ALU.subtract, ALU.mult).then_inc(xh_ready, 1)

            def values(b, par):
                dve.wait_ge(v_ps, b + 1)
                if not first(b, 2):
                    dve.wait_ge(pv, R * (b - 1))
                nc.vector.tensor_copy(vf[par], psVY[:, 0:D]).then_inc(v_ready, 1)

            def bias(b, r, par):
                n = R * b + r
                dve.wait_ge(s_ps, n + 1)
                if r == 0:
                    dve.wait_ge(dneg_done, b + 1)
                if not first(b):
                    dve.wait_ge(pt_ps, n - 3)
                for j in range(HR):
                    q = HR * r + j
                    ins = nc.vector.scalar_tensor_tensor(sc[r][:, j * T:(j + 1) * T], dneg[par], and_[:, q:q + 1],
                                                         psS[r % 2][:, j * T:(j + 1) * T], ALU.mult, ALU.add)
                ins.then_inc(biased, 1)

            def move_probs(b, r):
                if r not in MOVED_BY_VECTOR:
                    return
                n = R * b + r
                dve.wait_ge(pt_ps, n + 1)
                if not (first(b) and r < 2):
                    dve.wait_ge(pv, n - 1)
                nc.vector.tensor_copy(pT[r % 2], psT[r % 2][:]).then_inc(pt_dve, 1)

            def least(b, r, par):
                n = R * b + r
                if r in MIXED:
                    if not first(b):
                        dve.wait_ge(pt_ps, n - 3)
                dve.wait_ge(pb_ready, n + 1)
                if not first(b, 2):
                    dve.wait_ge(probs, n - 7)
                if r in MIXED:
                    wait_alone(dve, "dve", s_ps, n + 1)
                else:
                    wait_alone(dve, "dve", biased, biased_through(b, r))
                for j in range(HR):
                    s = sc[r][:, j * T:(j + 1) * T]
                    q = r * HR + j
                    ins = nc.vector.tensor_tensor_reduce(out=s, in0=psS[r % 2][:, j * T:(j + 1) * T] if r in MIXED else s,
                                                         in1=pb[r][:, j * T:(j + 1) * T], scale=1.0,
                                                         scalar=3.0e38, op0=ALU.add, op1=ALU.min, accum_out=mn[:, par, q:q + 1])
                ins.then_inc(scored, 1)

            def output(b, par):
                dve.wait_ge(pv, R * b + R)
                if not first(b):
                    dve.wait_ge(oT_ps, b)
                nc.vector.reciprocal(rs[:], sm[:, par, :]).then_inc(rs_done, 1)
                dve.wait_ge(rs_done, b + 1)
                for c in range(DC):
                    ins = nc.vector.tensor_tensor(
                        on[:, c * P:(c + 1) * P].rearrange("p (r e d) -> p r e d", r=R, e=2),
                        psO[:, c * P:(c + 1) * P].rearrange("p (r e d) -> p r e d", r=R, e=2),
                        rs[:].rearrange("p (r c e o) -> p c r e o", r=R, c=DC, o=1)[:, c].to_broadcast([P, R, 2, HD]),
                        ALU.mult)
                ins.then_inc(o_ready, 1)

            def residual(b):
                dve.wait_ge(y_ps, b + 1)
                dve.wait_ge(xb_ready, b + 1)
                xb = xres[:, bass.ds(b * D, D)]
                nc.vector.scalar_tensor_tensor(xb, psVY[:, D:2 * D], tgx[:, 0:1], xb, ALU.mult, ALU.add).then_inc(x1_ready, 1)
                wait_alone(dve, "dve", x1_ready, b + 1)
                nc.vector.bn_stats(st6[:, bass.ds(b, 1), :].rearrange("p b k -> p (b k)"), xb).then_inc(st_done, 1)

            def aggregate2(lo, hi):
                dve.wait_ge(st_done, hi)
                for b in range(lo, hi):
                    nc.vector.bn_aggr(mv2[:, b, :], st6[:, b, :]).then_inc(ln2_stat, 1)

            def seq(b, par):
                for r in range(R):
                    least(b, r, par)
                    if r == 2 and not first(b):
                        output(b - 1, 1 - par)
                    if not (first(b) and r == 0):
                        move_probs(*after(b, r, -1))
                    nb, nr = after(b, r, 1)
                    if nr not in MIXED and within(nb):
                        bias(nb, nr, par if nr else 1 - par)
                    if r == 1:
                        values(b, par)
                    if r == 3 and within(b + 2):
                        norm1(b + 2)
                    if r == 3 and not first(b, 2):
                        residual(b - 2)
                    if isinstance(b, int) and b == B - 1 and r == 0:
                        aggregate2(*LN2[0])
                    if first(b):
                        for k in range(4 + 3 * r, 7 + 3 * r):
                            stats1(k)

            for b in range(4):
                stats1(b)
            dve.wait_ge(ld_par, 48)
            link(nc.vector.tensor_scalar(gs[:], row[:, V_GAMMA:V_GAMMA + 1], -(HD ** -0.5), None, ALU.mult))
            link(nc.vector.tensor_scalar(bqs[:], col[:, K_BQ:K_BQ + DC], gs[:, 0:1], None, ALU.mult))
            for e in range(2):
                ins = nc.vector.tensor_scalar(bkm[:, e, :], col[:, K_BK:K_BK + DC], cst[:, C_EVEN + e:C_EVEN + e + 1], None, ALU.mult)
            ins.then_inc(setup_dve, 1)
            norm1(0)
            for t, v in ((apd, V_AP), (and_, V_AN)):
                for r in range(R):
                    ins = nc.vector.tensor_scalar(
                        t[:, HR * r:HR * (r + 1)].rearrange("p (c e) -> p c e", e=2),
                        row[:, v:v + H].rearrange("p (c r e) -> p r c e", c=DC, r=R)[:, r],
                        row[:, V_DELTA:V_DELTA + 1], -1.0, ALU.mult, ALU.mult)
            ins.then_inc(setup_dve, 1)
            norm1(1)
            bias(0, 0, 0)
            pairs(dve, seq)
            move_probs(B - 1, R - 1)
            gw = col[:, K_GW:K_GW + DC * E].rearrange("p (c e) -> p c e", c=DC)
            link(nc.vector.tensor_copy(gwhl[:, 0], gw))
            link(nc.vector.tensor_tensor(gwhl[:, 1], gw, gwhl[:, 0], ALU.subtract))
            nc.vector.tensor_copy(upb[:], cst[:, C_UP:C_UP + P])
            nc.vector.memset(oneb[:], 1.0)

            dve.wait_ge(ln2_rstd, 1)
            dve.wait_ge(pad_written, PADS)

            def norm2(i, k):
                if i >= 3:
                    dve.wait_ge(x2T_ps, i - 2)
                if 2 * i == LN2[1][0]:
                    dve.wait_ge(ln2_rstd, 2)
                for s in range(2):
                    b = 2 * i + s
                    ins = nc.vector.tensor_scalar(hbuf[:, k, s * D:(s + 1) * D], xres[:, bass.ds(b * D, D)], mv2[:, bass.ds(b, 1), 0],
                                                  rstd2[:, bass.ds(b, 1)], ALU.subtract, ALU.mult)
                ins.then_inc(xh2_ready, 1)

            def low2(i, k):
                dve.wait_ge(x2_hi, i + 1)
                xT = xT2[:, :].rearrange("p (k c n) -> p k c n", k=2, c=DC)
                nc.vector.tensor_tensor(xT[:, 1, :, bass.ds(i * 2 * T, 2 * T)],
                                        bank[k][:].rearrange("p (c t) -> p c t", c=DC),
                                        xT[:, 0, :, bass.ds(i * 2 * T, 2 * T)], ALU.subtract).then_inc(x2_lo, 1)

            for i in range(PAIRS):
                norm2(i, i % 3)
                if i == 0:
                    output(B - 1, 1)
                if i == 1:
                    residual(B - 2)
                if i >= 2:
                    low2(i - 2, (i - 2) % 3)
                if i == 2:
                    residual(B - 1)
                    aggregate2(*LN2[1])
            low2(PAIRS - 2, (PAIRS - 2) % 3)
            low2(PAIRS - 1, (PAIRS - 1) % 3)

            dve.wait_ge(gate_ps, B)
            link(nc.vector.tensor_tensor(lg, bank[5][:, 0:B * E].rearrange("p (b e) -> p b e", e=E),
                                         row[:, V_GB:V_GB + E].rearrange("p (o e) -> p o e", o=1).to_broadcast([P, B, E]), ALU.add))
            for b in range(B):
                ins = nc.vector.max(mx8[:, b, :], lg[:, b, :])
            link(ins)
            for b in range(B):
                ins = nc.vector.max_index(ix8[:, b, :], mx8[:, b, :], lg[:, b, :])
            link(ins)
            nc.vector.tensor_tensor(ed[:], mx8[:, :, 1], mx8[:, :, 0], ALU.subtract).then_inc(wd_ready, 1)
            link(nc.vector.tensor_copy(ixf[:], ix8[:, :, 0:TOPK]))
            iota = cst[:, C_IOTA:C_IOTA + E].rearrange("p (o e) -> p o e", o=1).to_broadcast([P, B, E])
            for k in range(TOPK):
                ins = nc.vector.tensor_tensor(oh[k], iota, ixf[:, :, k:k + 1].to_broadcast([P, B, E]), ALU.is_equal)
            link(ins)
            nc.vector.tensor_tensor(selm, oh[0], oh[1], ALU.add).then_inc(sel_ready, 1)
            dve.wait_ge(rank_ps, 1)
            nc.vector.tensor_copy(rank.rearrange("p k b e -> p (k b e)"), bank[4][:, 0:2 * B * E]).then_inc(ranks_read, 1)
            dve.wait_ge(ranks_read, 1)
            rows_before, cnt = rank[:, 0], rank[:, 1]
            link(nc.vector.tensor_copy(ca[0], cnt))
            a = 0
            step = 1
            while step < B:
                nc.vector.tensor_copy(ca[1 - a][:, 0:step, :], ca[a][:, 0:step, :])
                link(nc.vector.tensor_tensor(ca[1 - a][:, step:B, :], ca[a][:, step:B, :], ca[a][:, 0:B - step, :], ALU.add))
                a, step = 1 - a, 2 * step
            nc.vector.tensor_tensor(offs, ca[a], cnt, ALU.subtract)
            link(nc.vector.tensor_scalar(te_i[:], ca[a][:, B - 1, :], float(TR - 1), None, ALU.add))
            link(nc.vector.tensor_single_scalar(te_i[:], te_i[:], TR.bit_length() - 1, op=ALU.arith_shift_right))
            nc.vector.tensor_copy(te[0][:], te_i[:])
            link(nc.vector.tensor_copy(te[1][:], te_i[:]))
            k, step = 1, 1
            while step < E:
                nc.vector.tensor_copy(te[3 - k][:, 0:step], te[k][:, 0:step])
                link(nc.vector.tensor_tensor(te[3 - k][:, step:E], te[k][:, step:E], te[k][:, 0:E - step], ALU.add))
                k, step = 3 - k, 2 * step
            ends, base = te[k], te[3 - k]
            link(nc.vector.tensor_tensor(base[:], ends[:], te[0][:], ALU.subtract))
            link(nc.vector.tensor_scalar(base[:], base[:], float(TR), None, ALU.mult))
            link(nc.vector.tensor_tensor(offs, offs, rows_before, ALU.add))
            link(nc.vector.tensor_tensor(offs, offs, base[:].rearrange("p (o e) -> p o e", o=1).to_broadcast([P, B, E]), ALU.add))
            for k in range(TOPK):
                ins = nc.vector.tensor_tensor(ca[k], offs, oh[k], ALU.mult)
            link(ins)
            for k in range(TOPK):
                ins = nc.vector.tensor_reduce(posf[:, k, :], ca[k], AX.X, ALU.add)
            link(ins)
            link(nc.vector.tensor_copy(posu[:], posf[:]))
            dve.wait_ge(we_ready, 1)
            link(nc.vector.tensor_scalar(wt[:, :, 1], ed[:], 1.0, None, ALU.add))
            link(nc.vector.reciprocal(wt[:, :, 0], wt[:, :, 1]))
            link(nc.vector.tensor_tensor(wt[:, :, 1], ed[:], wt[:, :, 0], ALU.mult))
            nc.vector.tensor_scalar(wid[:, :, :, 0], wt[:], tgf[:, 0:1], None, ALU.mult)
            for k in range(TOPK):
                ins = nc.vector.tensor_copy(wid[:, :, k, 1], cst[:, C_TOK:C_TOK + B])
            link(ins)

            def payload(b):
                if b >= 4:
                    dve.wait_ge(dispatched[b % 4], 16 * TOPK * (b // 4))
                nc.vector.tensor_copy(place[:, b % 4, :], posu[:, :, b])
                for k in range(TOPK):
                    nc.vector.tensor_scalar(pay[:, b % 4, k, 0:D], xres[:, b * D:(b + 1) * D], mv2[:, b:b + 1, 0],
                                            rstd2[:, b:b + 1], ALU.subtract, ALU.mult)
                nc.vector.tensor_copy(pay[:, b % 4, :, D:ROW], wid[:, b]).then_inc(pay_ready, 1)

            def accumulate(g):
                dve.wait_ge(pay_ready, 4 * (g + 1))
                dve.wait_ge(sd_used, HC * (g + 1))
                for t in range(2):
                    xb = xres[:, (4 * g + 2 * t) * D:(4 * g + 2 * t + 2) * D]
                    ins = nc.vector.scalar_tensor_tensor(xb, bank[2 + 2 * (g % 2) + t][:], tgf[:, 0:1], xb, ALU.mult, ALU.add)
                ins.then_inc(acc_half, 1)
                dve.wait_ge(acc_half, g + 1)
                dve.wait_ge(setup_pool, 1)
                xb = xres[:, 4 * g * D:4 * (g + 1) * D].rearrange("p (t d) -> p t d", d=D)
                nc.vector.tensor_tensor(xb, xb, bs2t.rearrange("p (o d) -> p o d", o=1).to_broadcast([P, 4, D]), ALU.add).then_inc(acc_ready, 1)

            for b in range(4):
                payload(b)

            def tile_table():
                link(nc.vector.tensor_tensor(
                    tcmp, cst[:, C_TILE:C_TILE + TILES].rearrange("p (j o) -> p j o", o=1).to_broadcast([P, TILES, E]),
                    ends[:].rearrange("p (o e) -> p o e", o=1).to_broadcast([P, TILES, E]), ALU.is_ge))
                link(nc.vector.tensor_reduce(tef[:], tcmp, AX.X, ALU.add))
                nc.vector.tensor_scalar(tei[:], tef[:], float(E - 1), None, ALU.min).then_inc(routed, 1)

            for c in range(HC * GROUPS - POOL_SPLITS):
                m = POOL_SPLITS + c
                dve.wait_ge(sh_hi, m + 1)
                nc.vector.tensor_tensor(hsplit[:, m % DEEP, 1, :], hbuf[:, m % DEEP, :], hsplit[:, m % DEEP, 0, :],
                                        ALU.subtract).then_inc(sh_ready[1], 1)
                if m in ROWS_AT:
                    payload(4 + ROWS_AT.index(m))
                if m in LOWS_AT:
                    q = VECTOR_PIECES[LOWS_AT.index(m)]
                    at = piece_at(q // 2, q % 2)
                    dve.wait_ge(conv_hi, q + 1)
                    nc.vector.tensor_tensor(W[:, at + DC * HID:at + (DC + 1) * HID], stage[:, q % 2 * HID:(q % 2 + 1) * HID],
                                            W[:, at:at + HID], ALU.subtract).then_inc(converted_v, 1)
                if c == 0:
                    tile_table()
                if m % HC == 1:
                    accumulate(m // HC - 1)

            def bias_tile(j, par):
                e = dve.value_load(tei[0:1, bass.ds(j, 1)], min_val=0, max_val=E - 1)
                if not first(j, 2):
                    dve.wait_ge(g_ready, 4 * (j - 1))
                nc.vector.tensor_copy(b1t[:, par, :], col[:, bass.ds(K_B1 + e * HC, HC)]).then_inc(b1_ready, 1)

            def low_tile(j, par):
                dve.wait_ge(xs_hi, j + 1)
                if not first(j, 2):
                    dve.wait_ge(up_ps, 4 * (j - 1))
                nc.vector.tensor_tensor(xsT[par][:, DC * TR:2 * DC * TR], bank[6 + par][:, 0:DC * TR], xsT[par][:, 0:DC * TR],
                                        ALU.subtract).then_inc(xs_lo, 1)

            def split_tile(j, par):
                for q in range(4):
                    dve.wait_ge(g_ready, 4 * j + q + 1)
                    if q == 0 and not first(j, 2):
                        dve.wait_ge(down_ps, j - 1)
                    hi = hs[par][:, 2 * q * TR:2 * (q + 1) * TR]
                    lo = hs[par][:, (HC + 2 * q) * TR:(HC + 2 * q + 2) * TR]
                    nc.vector.tensor_copy(hi, hbuf[:, q % 2, :]).then_inc(h_hi, 1)
                    dve.wait_ge(h_hi, 4 * j + q + 1)
                    nc.vector.tensor_tensor(lo, hbuf[:, q % 2, :], hi, ALU.subtract).then_inc(h_ready, 1)

            def weigh(j, par):
                e = dve.value_load(tei[0:1, bass.ds(j, 1)], min_val=0, max_val=E - 1)
                dve.wait_ge(down_ps, j + 1)
                if first(j):
                    dve.wait_ge(ld_b2, 16)
                if not first(j, 2):
                    dve.wait_ge(added[TH - 1], 16 * (j - 1))
                m = meta[:, bass.ds(j * TH, TH), :]
                both = xres[:, GD + TH * par * D:GD + TH * (par + 1) * D].rearrange("p (t d) -> p t d", d=D)
                nc.vector.tensor_tensor(both, bank[4 + par][:].rearrange("p (t d) -> p t d", d=D),
                                        b2f[:, bass.ds(e * D, D)].rearrange("p (o d) -> p o d", o=1).to_broadcast([P, TH, D]),
                                        ALU.add).then_inc(biased_y, 1)
                nc.vector.tensor_copy(idu[:, par, :], m[:, :, 1])
                wait_alone(dve, "dve", biased_y, j + 1)
                for t in range(TH):
                    ins = nc.vector.tensor_scalar(ysb[par][t], ysb[par][t], m[:, t, 0:1], None, ALU.mult)
                ins.then_inc(y_ready, 1)

            def body(j, par, more):
                if more:
                    bias_tile(j + 1, 1 - par)
                split_tile(j, par)
                if more == 2:
                    low_tile(j + 2, par)
                if not first(j):
                    weigh(j - 1, 1 - par)

            bias_tile(0, 0)
            low_tile(0, 0)
            low_tile(1, 1)
            accumulate(3)
            dve.wait_ge(meta_in, 16)
            dve.wait_ge(out_written[1], 16)
            tiles(dve, body)
            weigh(TILES - 1, (TILES - 1) % 2)

        @block.tensor
        def _(pe):
            def mm(o, a, b, start, stop, **kw):
                return nc.tensor.matmul(o, a, b, start=start, stop=stop, **kw)

            def turn_xh(b):
                pe.wait_ge(xh_ready, b + 1)
                if not first(b, 3):
                    pe.wait_ge(oT_ready, b - 2)
                elif not first(b):
                    pe.wait_ge(xhT_ready, b)
                for c in range(DC):
                    ins = nc.tensor.transpose(psM[:, c * T:(c + 1) * T], xh[:, c * P:(c + 1) * P], ident)
                ins.then_inc(xhT_ps, 1)

            def project(k, b, src, done):
                for o in range(DC):
                    for c in range(DC):
                        ins = mm(psQK[:, (k * DC + o) * T:(k * DC + o + 1) * T], wproj_at(k, c)[:, o * P:(o + 1) * P],
                                 src[:, c * T:(c + 1) * T], c == 0, c == DC - 1)
                ins.then_inc(done, 1)

            def project_k(b, par):
                pe.wait_ge(ld_ctx[par], 32 * (b // 2 + 1) if isinstance(b, int) else 16 * (b - par) + 32)
                if not first(b):
                    pe.wait_ge(q_ready, b)
                project(1, b, cT[par], k_ps)

            def project_q(b):
                pe.wait_ge(xhT_ready, b + 1)
                pe.wait_ge(k_ready, b + 1)
                project(0, b, xhT, q_ps)

            def project_v(b, par):
                if not first(b, 3):
                    pe.wait_ge(x1_ready, b - 2)
                if not first(b):
                    pe.wait_ge(v_ready, b)
                for c in range(DC):
                    ins = mm(psVY[:, 0:D], cT[par][:, c * T:(c + 1) * T], wproj_at(2, c), c == 0, c == DC - 1)
                ins.then_inc(v_ps, 1)

            def scores(b, r, par):
                if r == 0:
                    pe.wait_ge(q_ready, b + 1)
                    pe.wait_ge(k_ready, b + 1)
                if not (first(b) and r < 2):
                    scores_read(pe, *after(b, r, -2))
                rows = slice(32 * r, 32 * r + 32)
                for j in range(HR):
                    c, e = j // 2, j % 2
                    ins = mm(psS[r % 2][:, j * T:(j + 1) * T], qT[par][rows, c * T:(c + 1) * T],
                             kz[par][rows, (e * DC + c) * T:(e * DC + c + 1) * T], True, True)
                ins.then_inc(s_ps, 1)

            def turn_probs(n, r, b):
                pe.wait_ge(probs, n + 1)
                if not (first(b) and r < 2):
                    moved(pe, *after(b, r, -2))
                for j in range(HR):
                    ins = nc.tensor.transpose(psT[r % 2][:, j * T:(j + 1) * T], sc[r][:, j * T:(j + 1) * T], ident)
                ins.then_inc(pt_ps, 1)

            def weigh_values(b, r, par):
                moved(pe, b, r)
                if r == 0:
                    pe.wait_ge(v_ready, b + 1)
                    if not first(b):
                        pe.wait_ge(o_ready, b)
                for j in range(HR):
                    h = head(r, j)
                    ins = mm(psO[:, h * HD:(h + 1) * HD], pT[r % 2][:, j * T:(j + 1) * T], vf[par][:, h * HD:(h + 1) * HD], True, True)
                ins.then_inc(pv, 1)

            def turn_o(b):
                pe.wait_ge(o_ready, b + 1)
                pe.wait_ge(xhT_ready, b + 3 if within(b + 2) else B)
                for c in range(DC):
                    ins = nc.tensor.transpose(psM[:, c * T:(c + 1) * T], on[:, c * P:(c + 1) * P], ident)
                ins.then_inc(oT_ps, 1)

            def project_o(b):
                pe.wait_ge(oT_ready, b + 1)
                pe.wait_ge(v_ready, b + 3 if within(b + 2) else B)
                if not first(b):
                    pe.wait_ge(x1_ready, b)
                for c in range(DC):
                    ins = mm(psVY[:, D:2 * D], oT[:, c * T:(c + 1) * T], wproj_at(3, c), c == 0, c == DC - 1)
                ins.then_inc(y_ps, 1)

            def seq(b, par):
                for r in range(R):
                    n = R * b + r
                    nb, nr = after(b, r, 2)
                    if within(nb):
                        scores(nb, nr, par if r < 2 else 1 - par)
                    if r >= 2:
                        weigh_values(b, r - 2, par)
                    elif not first(b):
                        weigh_values(b - 1, r + 2, 1 - par)
                    turn_probs(n, r, b)
                    if r == 0 and within(b + 1):
                        project_q(b + 1)
                    if r == 1 and not first(b, 2):
                        project_o(b - 2)
                    if r == 2 and not first(b):
                        turn_o(b - 1)
                    if r == 2 and within(b + 2):
                        project_k(b + 2, par)
                    if r == 3 and within(b + 2):
                        turn_xh(b + 2)
                    if r == 3 and within(b + 1):
                        project_v(b + 1, 1 - par)

            pe.wait_ge(ld_wp[1], 16)
            project_k(0, 0)
            pe.wait_ge(ld_wp[2], 16)
            project_v(0, 0)
            pe.wait_ge(ld_par, 48)
            turn_xh(0)
            pe.wait_ge(ld_wp[0], 16)
            project_q(0)
            turn_xh(1)
            project_k(1, 1)
            scores(0, 0, 0)
            scores(0, 1, 0)
            pe.wait_ge(ld_wp[3], 16)
            pairs(pe, seq)
            weigh_values(B - 1, 2, 1)
            weigh_values(B - 1, 3, 1)

            def turn2(i, k):
                pe.wait_ge(xh2_ready, i + 1)
                if i >= 3:
                    pe.wait_ge(x2_lo, i - 2)
                for c in range(DC):
                    for s in range(2):
                        ins = nc.tensor.transpose(bank[k][:, (c * 2 + s) * T:(c * 2 + s + 1) * T],
                                                  hbuf[:, k, s * D + c * P:s * D + (c + 1) * P], ident)
                ins.then_inc(x2T_ps, 1)

            def gate(i):
                pe.wait_ge(x2_lo, i + 1)
                for s in range(2):
                    b = 2 * i + s
                    for c in range(DC):
                        for p in range(4):
                            ins = mm(bank[5][:, bass.ds(b * E, E)], xT2[:, bass.ds((p % 2) * DC * N + c * N + b * T, T)],
                                     gwhl[:, p // 2, c, :], c == 0 and p == 0, c == DC - 1 and p == 3)
                    ins.then_inc(gate_ps, 1)

            for i in range(PAIRS):
                if i == 1:
                    turn_o(B - 1)
                if i == 2:
                    project_o(B - 1)
                turn2(i, i % 3)
                if i == 1:
                    project_o(B - 2)
                if i >= 3:
                    gate(i - 3)
            for i in range(PAIRS - 3, PAIRS):
                gate(i)

            def w_up(base, part, c, j):
                return W[:, bass.ds(base + (W1L if part else W1H) + c * HID + j * P, P)]

            def w_down(base, part, j):
                return W[:, bass.ds(base + (W2L if part else W2H) + j * D, D)]

            def shared_up(m):
                g, j = m // HC, m % HC
                if m >= DEEP:
                    pe.wait_ge(sg_ready, m - DEEP + 1)
                n = 0
                for wpart, xpart in ((0, 0), (1, 0), (0, 1)):
                    for c in range(DC):
                        at = xpart * DC * N + c * N + g * 512
                        ins = mm(bank[(0, 1, 7)[m % DEEP]][:], w_up(0, wpart, c, j), xT2[:, at:at + 512], n == 0, n == 5)
                        n += 1
                ins.then_inc(su_ps, 1)

            def shared_down(m):
                g, j = m // HC, m % HC
                split_ready(pe, m)
                if j == 0 and g == 1:
                    pe.wait_ge(ranks_read, 1)
                if j == 0 and g > 1:
                    pe.wait_ge(acc_half, g - 1)
                n = 0
                for hpart, wpart in ((0, 0), (0, 1), (1, 0)):
                    for t in range(4):
                        ins = mm(bank[2 + 2 * (g % 2) + t // 2][:, (t % 2) * D:(t % 2 + 1) * D],
                                 hsplit[:, m % DEEP, hpart, t * P:(t + 1) * P], w_down(0, wpart, j),
                                 j == 0 and n == 0 and t % 2 == 0, j == HC - 1 and n == 2, skip_group_check=True)
                    n += 1
                ins.then_inc(sd_used, 1)

            def turn_tile(j, par):
                pe.wait_ge(xs_in[par], 16 * (j // 2) + 16 if isinstance(j, int) else 8 * (j - par) + 16)
                if not first(j, 2):
                    pe.wait_ge(xs_lo, j - 1)
                for t in range(TH):
                    for c in range(DC):
                        ins = nc.tensor.transpose(bank[6 + par][:, (c * TH + t) * P:(c * TH + t + 1) * P],
                                                  xs[par][:, (t * DC + c) * P:(t * DC + c + 1) * P], ident)
                ins.then_inc(xsT_ps, 1)

            piece_converted(pe, 3)
            shared_up(0)
            shared_up(1)
            for m in range(HC * GROUPS):
                if m + 2 < HC * GROUPS:
                    shared_up(m + 2)
                if m == 1:
                    pe.wait_ge(sel_ready, 1)
                    sel = selm.rearrange("p b e -> p (b e)")
                    mm(bank[4][:, 0:B * E], upb[:], sel, True, True)
                    mm(bank[4][:, B * E:2 * B * E], oneb[:], sel, True, True).then_inc(rank_ps, 1)
                if m == HC * GROUPS - 2:
                    turn_tile(0, 0)
                if m == HC * GROUPS - 1:
                    pe.wait_ge(sg_ready, HC * GROUPS)
                    turn_tile(1, 1)
                shared_down(m)

            def base_of(j):
                e = pe.value_load(tei[0:1, bass.ds(j, 1)], min_val=0, max_val=E - 1)
                return (e + 1) * WS

            def up_tile(j, par):
                base = base_of(j)
                pe.wait_ge(xs_lo, j + 1)
                for q in range(4):
                    if not first(j):
                        pe.wait_ge(g_ready, 4 * (j - 1) + q + 1)
                    elif q == 2:
                        pe.wait_ge(acc_half, GROUPS - 1)
                    for h in range(2):
                        n = 0
                        for wpart, xpart in ((0, 0), (0, 1), (1, 0)):
                            for c in range(DC):
                                ins = mm(bank[q][:, h * TR:(h + 1) * TR], w_up(base, wpart, c, 2 * q + h),
                                         xsT[par][:, (xpart * DC + c) * TR:(xpart * DC + c + 1) * TR], n == 0, n == 5)
                                n += 1
                    ins.then_inc(up_ps, 1)

            def down_tile(j, par):
                base = base_of(j)
                if not first(j, 2):
                    pe.wait_ge(y_ready, j - 1)
                else:
                    pe.wait_ge(acc_half, GROUPS)
                y = [bank[4 + par][:, t * D:(t + 1) * D] for t in range(TH)]
                for c in range(HC):
                    if c % 2 == 0:
                        pe.wait_ge(h_ready, 4 * j + c // 2 + 1)
                    for hpart, wpart in ((0, 0), (1, 0), (0, 1)):
                        for t in range(TH):
                            at = (hpart * HC + c) * TR + t * P
                            ins = mm(y[t], hs[par][:, at:at + P], w_down(base, wpart, c),
                                     c == 0 and hpart == 0 and wpart == 0 and t == 0, c == HC - 1 and wpart == 1, skip_group_check=True)
                ins.then_inc(down_ps, 1)

            def body(j, par, more):
                up_tile(j, par)
                if more == 2:
                    turn_tile(j + 2, par)
                if not first(j):
                    down_tile(j - 1, 1 - par)
                if isinstance(j, int) and j == 1:
                    piece_converted(pe, PIECES - 1)

            piece_converted(pe, VECTOR_PIECES[0] - 1)
            piece_converted(pe, VECTOR_PIECES[-1])
            tiles(pe, body)
            down_tile(TILES - 1, (TILES - 1) % 2)


def kernel(**inputs):
    import numpy as np
    import concourse.bacc as bacc
    from concourse.bass_utils import run_bass_kernel_spmd

    def a(name):
        return np.asarray(inputs[name], order="C")

    def chunks(v):
        return v.reshape(-1, P).T

    f = np.float32
    x = a("x")
    ctxT = np.ascontiguousarray(a("ctx_1024").reshape(N, D).T.reshape(DC, P, N))
    frac = np.ascontiguousarray(a("fside_BxS2_0").reshape(1, N))
    wproj = np.stack([a(f"L0_xattn_W{k}").T for k in "qkvo"])
    p = np.arange(P)
    consts = np.concatenate([
        np.eye(P), p[:, None] < p[None, :],
        np.stack([p % 32 < HD, p % 32 >= HD], 1),
        np.tile(np.arange(E), (P, 1)), p[:, None] + T * np.arange(B)[None], N + p[:, None] + P * np.arange(TH)[None],
        np.tile(np.arange(TILES), (P, 1))], axis=1).astype(f)
    cols = np.concatenate([
        chunks(a("L0_xattn_bq")), chunks(a("L0_xattn_bk")), chunks(a("L0_xattn_bv")),
        a("fside_BxS2_0").T, chunks(a("L0_ffn_bs1")),
        a("L0_ffn_b1").reshape(E, HC, P).transpose(2, 0, 1).reshape(P, E * HC),
        a("L0_ffn_gate_w").reshape(DC, P, E).transpose(1, 0, 2).reshape(P, DC * E)], axis=1)
    rows = np.concatenate([
        a("L0_xattn_alpha_pos"), a("L0_xattn_alpha_neg"), a("L0_xattn_gamma").reshape(1),
        a("L0_xattn_delta").reshape(1), a("g_xattn").reshape(1), a("g_ffn").reshape(1),
        a("L0_ffn_gate_b"), a("L0_xattn_bo"), a("L0_ffn_bs2")])[None]
    b2 = a("L0_ffn_b2").reshape(1, E * D)
    w1 = np.concatenate([a("L0_ffn_ws1")[None], a("L0_ffn_w1")]).reshape(1 + E, DC, P, HID)
    w2 = np.concatenate([a("L0_ffn_ws2")[None], a("L0_ffn_w2")]).reshape(1 + E, 2, HC // 2, P, D)
    wts = np.concatenate([w1, w2.transpose(0, 1, 3, 2, 4).reshape(1 + E, 2, P, HID)], axis=1).reshape(PIECES * P, HID)

    nc = bacc.Bacc("TRN2", target_bir_lowering=False, num_devices=1)
    arrays, args = {}, []
    for name, v in dict(x=x, ctxT=ctxT, frac=frac, wproj=wproj, consts=consts, cols=cols, rows=rows,
                        b2=b2, wts=wts).items():
        arrays[name] = np.ascontiguousarray(v)
        args.append(nc.dram_tensor(name, v.shape, mybir.dt.from_np(v.dtype), kind="ExternalInput").ap())
    xs_dram = nc.dram_tensor("xs_dram", (TILES * TR, ROW), mybir.dt.float32).ap()
    out = nc.dram_tensor("out", (N + TR, D), mybir.dt.float32, kind="ExternalOutput").ap()
    build(nc, *args, xs_dram, out)
    r = run_bass_kernel_spmd(nc, [arrays], core_ids=[0])
    return r.results[0]["out"][:N].reshape(B, T, D)
```
